# Optimizing a Trainium2 kernel written in Bass

```python
import numpy as np
import jax
import jax.numpy as jnp

def _softmax(x, axis=-1):
    return jax.nn.softmax(x, axis=axis)

def _gelu(x):
    return jax.nn.gelu(x, approximate=True)

def _silu(x):
    return jax.nn.silu(x)

def _sigmoid(x):
    return jax.nn.sigmoid(x)

def _layernorm(x, axis=-1, eps=1e-05):
    m = jnp.mean(x, axis=axis, keepdims=True)
    v = jnp.var(x, axis=axis, keepdims=True)
    return (x - m) / jnp.sqrt(v + eps)

def _scatter_add(tgt, idx, src, axis=0):
    return tgt.at[idx].add(src)

def _segment_sum(src, seg, n):
    return jax.ops.segment_sum(src, seg, n)
kernel_name = 'mk_rec_standalone_d1_rec_r8_7afc72'

def setup_inputs(seed: int=0):
    np.random.seed(seed)
    _w = jnp.asarray

    def _rec_inputs():
        import jax
        import jax.numpy as jnp
        _rk = jax.random.key(seed)
        r_item_seq = jnp.stack([jax.random.randint(jax.random.fold_in(jax.random.fold_in(_rk, 1), 0), (512,), 171, 99919, jnp.int32), jax.random.randint(jax.random.fold_in(jax.random.fold_in(_rk, 1), 1), (512,), 22, 99993, jnp.int32), jax.random.randint(jax.random.fold_in(jax.random.fold_in(_rk, 1), 2), (512,), 29, 99986, jnp.int32), jax.random.randint(jax.random.fold_in(jax.random.fold_in(_rk, 1), 3), (512,), 67, 99929, jnp.int32), jax.random.randint(jax.random.fold_in(jax.random.fold_in(_rk, 1), 4), (512,), 68, 99930, jnp.int32), jax.random.randint(jax.random.fold_in(jax.random.fold_in(_rk, 1), 5), (512,), 167, 99906, jnp.int32), jax.random.randint(jax.random.fold_in(jax.random.fold_in(_rk, 1), 6), (512,), 161, 99809, jnp.int32), jax.random.randint(jax.random.fold_in(jax.random.fold_in(_rk, 1), 7), (512,), 32, 99925, jnp.int32), jax.random.randint(jax.random.fold_in(jax.random.fold_in(_rk, 1), 8), (512,), 66, 99957, jnp.int32), jax.random.randint(jax.random.fold_in(jax.random.fold_in(_rk, 1), 9), (512,), 13, 99926, jnp.int32), jax.random.randint(jax.random.fold_in(jax.random.fold_in(_rk, 1), 10), (512,), 387, 99756, jnp.int32), jax.random.randint(jax.random.fold_in(jax.random.fold_in(_rk, 1), 11), (512,), 146, 99961, jnp.int32), jax.random.randint(jax.random.fold_in(jax.random.fold_in(_rk, 1), 12), (512,), 80, 99998, jnp.int32), jax.random.randint(jax.random.fold_in(jax.random.fold_in(_rk, 1), 13), (512,), 348, 99970, jnp.int32), jax.random.randint(jax.random.fold_in(jax.random.fold_in(_rk, 1), 14), (512,), 182, 99931, jnp.int32), jax.random.randint(jax.random.fold_in(jax.random.fold_in(_rk, 1), 15), (512,), 94, 99939, jnp.int32), jax.random.randint(jax.random.fold_in(jax.random.fold_in(_rk, 1), 16), (512,), 28, 99982, jnp.int32), jax.random.randint(jax.random.fold_in(jax.random.fold_in(_rk, 1), 17), (512,), 4, 99942, jnp.int32), jax.random.randint(jax.random.fold_in(jax.random.fold_in(_rk, 1), 18), (512,), 50, 99806, jnp.int32), jax.random.randint(jax.random.fold_in(jax.random.fold_in(_rk, 1), 19), (512,), 15, 12488, jnp.int32), jax.random.randint(jax.random.fold_in(jax.random.fold_in(_rk, 1), 20), (512,), 78, 99909, jnp.int32), jax.random.randint(jax.random.fold_in(jax.random.fold_in(_rk, 1), 21), (512,), 131, 99977, jnp.int32), jax.random.randint(jax.random.fold_in(jax.random.fold_in(_rk, 1), 22), (512,), 226, 99927, jnp.int32), jax.random.randint(jax.random.fold_in(jax.random.fold_in(_rk, 1), 23), (512,), 203, 99919, jnp.int32), jax.random.randint(jax.random.fold_in(jax.random.fold_in(_rk, 1), 24), (512,), 126, 99953, jnp.int32), jax.random.randint(jax.random.fold_in(jax.random.fold_in(_rk, 1), 25), (512,), 35, 99942, jnp.int32), jax.random.randint(jax.random.fold_in(jax.random.fold_in(_rk, 1), 26), (512,), 163, 99927, jnp.int32), jax.random.randint(jax.random.fold_in(jax.random.fold_in(_rk, 1), 27), (512,), 104, 99987, jnp.int32), jax.random.randint(jax.random.fold_in(jax.random.fold_in(_rk, 1), 28), (512,), 138, 99993, jnp.int32), jax.random.randint(jax.random.fold_in(jax.random.fold_in(_rk, 1), 29), (512,), 78, 99946, jnp.int32), jax.random.randint(jax.random.fold_in(jax.random.fold_in(_rk, 1), 30), (512,), 230, 99874, jnp.int32), jax.random.randint(jax.random.fold_in(jax.random.fold_in(_rk, 1), 31), (512,), 69, 99871, jnp.int32), jax.random.randint(jax.random.fold_in(jax.random.fold_in(_rk, 1), 32), (512,), 30, 99909, jnp.int32), jax.random.randint(jax.random.fold_in(jax.random.fold_in(_rk, 1), 33), (512,), 47, 99949, jnp.int32), jax.random.randint(jax.random.fold_in(jax.random.fold_in(_rk, 1), 34), (512,), 8, 99967, jnp.int32), jax.random.randint(jax.random.fold_in(jax.random.fold_in(_rk, 1), 35), (512,), 60, 99998, jnp.int32), jax.random.randint(jax.random.fold_in(jax.random.fold_in(_rk, 1), 36), (512,), 275, 99938, jnp.int32), jax.random.randint(jax.random.fold_in(jax.random.fold_in(_rk, 1), 37), (512,), 54, 12497, jnp.int32), jax.random.randint(jax.random.fold_in(jax.random.fold_in(_rk, 1), 38), (512,), 27, 99995, jnp.int32), jax.random.randint(jax.random.fold_in(jax.random.fold_in(_rk, 1), 39), (512,), 14, 12493, jnp.int32), jax.random.randint(jax.random.fold_in(jax.random.fold_in(_rk, 1), 40), (512,), 20, 99980, jnp.int32), jax.random.randint(jax.random.fold_in(jax.random.fold_in(_rk, 1), 41), (512,), 33, 12464, jnp.int32), jax.random.randint(jax.random.fold_in(jax.random.fold_in(_rk, 1), 42), (512,), 51, 99990, jnp.int32), jax.random.randint(jax.random.fold_in(jax.random.fold_in(_rk, 1), 43), (512,), 45, 99982, jnp.int32), jax.random.randint(jax.random.fold_in(jax.random.fold_in(_rk, 1), 44), (512,), 86, 99993, jnp.int32), jax.random.randint(jax.random.fold_in(jax.random.fold_in(_rk, 1), 45), (512,), 246, 99925, jnp.int32), jax.random.randint(jax.random.fold_in(jax.random.fold_in(_rk, 1), 46), (512,), 300, 99831, jnp.int32), jax.random.randint(jax.random.fold_in(jax.random.fold_in(_rk, 1), 47), (512,), 95, 12494, jnp.int32), jax.random.randint(jax.random.fold_in(jax.random.fold_in(_rk, 1), 48), (512,), 156, 99964, jnp.int32), jax.random.randint(jax.random.fold_in(jax.random.fold_in(_rk, 1), 49), (512,), 21, 99979, jnp.int32), jax.random.randint(jax.random.fold_in(jax.random.fold_in(_rk, 1), 50), (512,), 224, 99942, jnp.int32), jax.random.randint(jax.random.fold_in(jax.random.fold_in(_rk, 1), 51), (512,), 245, 12494, jnp.int32), jax.random.randint(jax.random.fold_in(jax.random.fold_in(_rk, 1), 52), (512,), 281, 99966, jnp.int32), jax.random.randint(jax.random.fold_in(jax.random.fold_in(_rk, 1), 53), (512,), 11, 12476, jnp.int32), jax.random.randint(jax.random.fold_in(jax.random.fold_in(_rk, 1), 54), (512,), 159, 99948, jnp.int32), jax.random.randint(jax.random.fold_in(jax.random.fold_in(_rk, 1), 55), (512,), 83, 99942, jnp.int32), jax.random.randint(jax.random.fold_in(jax.random.fold_in(_rk, 1), 56), (512,), 1, 99971, jnp.int32), jax.random.randint(jax.random.fold_in(jax.random.fold_in(_rk, 1), 57), (512,), 31, 99986, jnp.int32), jax.random.randint(jax.random.fold_in(jax.random.fold_in(_rk, 1), 58), (512,), 128, 99996, jnp.int32), jax.random.randint(jax.random.fold_in(jax.random.fold_in(_rk, 1), 59), (512,), 72, 99983, jnp.int32), jax.random.randint(jax.random.fold_in(jax.random.fold_in(_rk, 1), 60), (512,), 127, 12483, jnp.int32), jax.random.randint(jax.random.fold_in(jax.random.fold_in(_rk, 1), 61), (512,), 181, 99826, jnp.int32), jax.random.randint(jax.random.fold_in(jax.random.fold_in(_rk, 1), 62), (512,), 231, 12480, jnp.int32), jax.random.randint(jax.random.fold_in(jax.random.fold_in(_rk, 1), 63), (512,), 31, 99973, jnp.int32), jax.random.randint(jax.random.fold_in(jax.random.fold_in(_rk, 1), 64), (512,), 51, 99970, jnp.int32), jax.random.randint(jax.random.fold_in(jax.random.fold_in(_rk, 1), 65), (512,), 42, 99919, jnp.int32), jax.random.randint(jax.random.fold_in(jax.random.fold_in(_rk, 1), 66), (512,), 40, 99913, jnp.int32), jax.random.randint(jax.random.fold_in(jax.random.fold_in(_rk, 1), 67), (512,), 20, 99962, jnp.int32), jax.random.randint(jax.random.fold_in(jax.random.fold_in(_rk, 1), 68), (512,), 11, 12488, jnp.int32), jax.random.randint(jax.random.fold_in(jax.random.fold_in(_rk, 1), 69), (512,), 121, 99907, jnp.int32), jax.random.randint(jax.random.fold_in(jax.random.fold_in(_rk, 1), 70), (512,), 1, 99882, jnp.int32), jax.random.randint(jax.random.fold_in(jax.random.fold_in(_rk, 1), 71), (512,), 325, 99994, jnp.int32), jax.random.randint(jax.random.fold_in(jax.random.fold_in(_rk, 1), 72), (512,), 129, 12481, jnp.int32), jax.random.randint(jax.random.fold_in(jax.random.fold_in(_rk, 1), 73), (512,), 226, 99861, jnp.int32), jax.random.randint(jax.random.fold_in(jax.random.fold_in(_rk, 1), 74), (512,), 5, 99930, jnp.int32), jax.random.randint(jax.random.fold_in(jax.random.fold_in(_rk, 1), 75), (512,), 2, 99978, jnp.int32), jax.random.randint(jax.random.fold_in(jax.random.fold_in(_rk, 1), 76), (512,), 40, 99911, jnp.int32), jax.random.randint(jax.random.fold_in(jax.random.fold_in(_rk, 1), 77), (512,), 15, 12493, jnp.int32), jax.random.randint(jax.random.fold_in(jax.random.fold_in(_rk, 1), 78), (512,), 44, 99993, jnp.int32), jax.random.randint(jax.random.fold_in(jax.random.fold_in(_rk, 1), 79), (512,), 53, 99990, jnp.int32), jax.random.randint(jax.random.fold_in(jax.random.fold_in(_rk, 1), 80), (512,), 111, 99983, jnp.int32), jax.random.randint(jax.random.fold_in(jax.random.fold_in(_rk, 1), 81), (512,), 116, 99810, jnp.int32), jax.random.randint(jax.random.fold_in(jax.random.fold_in(_rk, 1), 82), (512,), 163, 99750, jnp.int32), jax.random.randint(jax.random.fold_in(jax.random.fold_in(_rk, 1), 83), (512,), 172, 99991, jnp.int32), jax.random.randint(jax.random.fold_in(jax.random.fold_in(_rk, 1), 84), (512,), 171, 12478, jnp.int32), jax.random.randint(jax.random.fold_in(jax.random.fold_in(_rk, 1), 85), (512,), 19, 99949, jnp.int32), jax.random.randint(jax.random.fold_in(jax.random.fold_in(_rk, 1), 86), (512,), 148, 99948, jnp.int32), jax.random.randint(jax.random.fold_in(jax.random.fold_in(_rk, 1), 87), (512,), 68, 99893, jnp.int32), jax.random.randint(jax.random.fold_in(jax.random.fold_in(_rk, 1), 88), (512,), 38, 99881, jnp.int32), jax.random.randint(jax.random.fold_in(jax.random.fold_in(_rk, 1), 89), (512,), 10, 99925, jnp.int32), jax.random.randint(jax.random.fold_in(jax.random.fold_in(_rk, 1), 90), (512,), 109, 99937, jnp.int32), jax.random.randint(jax.random.fold_in(jax.random.fold_in(_rk, 1), 91), (512,), 1, 99946, jnp.int32), jax.random.randint(jax.random.fold_in(jax.random.fold_in(_rk, 1), 92), (512,), 103, 99905, jnp.int32), jax.random.randint(jax.random.fold_in(jax.random.fold_in(_rk, 1), 93), (512,), 304, 99980, jnp.int32), jax.random.randint(jax.random.fold_in(jax.random.fold_in(_rk, 1), 94), (512,), 87, 99967, jnp.int32), jax.random.randint(jax.random.fold_in(jax.random.fold_in(_rk, 1), 95), (512,), 294, 99626, jnp.int32), jax.random.randint(jax.random.fold_in(jax.random.fold_in(_rk, 1), 96), (512,), 85, 99860, jnp.int32), jax.random.randint(jax.random.fold_in(jax.random.fold_in(_rk, 1), 97), (512,), 10, 99910, jnp.int32), jax.random.randint(jax.random.fold_in(jax.random.fold_in(_rk, 1), 98), (512,), 336, 12494, jnp.int32), jax.random.randint(jax.random.fold_in(jax.random.fold_in(_rk, 1), 99), (512,), 10, 99951, jnp.int32), jax.random.randint(jax.random.fold_in(jax.random.fold_in(_rk, 1), 100), (512,), 76, 99975, jnp.int32), jax.random.randint(jax.random.fold_in(jax.random.fold_in(_rk, 1), 101), (512,), 55, 99802, jnp.int32), jax.random.randint(jax.random.fold_in(jax.random.fold_in(_rk, 1), 102), (512,), 36, 99778, jnp.int32), jax.random.randint(jax.random.fold_in(jax.random.fold_in(_rk, 1), 103), (512,), 79, 99987, jnp.int32), jax.random.randint(jax.random.fold_in(jax.random.fold_in(_rk, 1), 104), (512,), 28, 99969, jnp.int32), jax.random.randint(jax.random.fold_in(jax.random.fold_in(_rk, 1), 105), (512,), 36, 99742, jnp.int32), jax.random.randint(jax.random.fold_in(jax.random.fold_in(_rk, 1), 106), (512,), 400, 99965, jnp.int32), jax.random.randint(jax.random.fold_in(jax.random.fold_in(_rk, 1), 107), (512,), 45, 99953, jnp.int32), jax.random.randint(jax.random.fold_in(jax.random.fold_in(_rk, 1), 108), (512,), 36, 99951, jnp.int32), jax.random.randint(jax.random.fold_in(jax.random.fold_in(_rk, 1), 109), (512,), 15, 99882, jnp.int32), jax.random.randint(jax.random.fold_in(jax.random.fold_in(_rk, 1), 110), (512,), 34, 99839, jnp.int32), jax.random.randint(jax.random.fold_in(jax.random.fold_in(_rk, 1), 111), (512,), 409, 99965, jnp.int32), jax.random.randint(jax.random.fold_in(jax.random.fold_in(_rk, 1), 112), (512,), 39, 99990, jnp.int32), jax.random.randint(jax.random.fold_in(jax.random.fold_in(_rk, 1), 113), (512,), 93, 99821, jnp.int32), jax.random.randint(jax.random.fold_in(jax.random.fold_in(_rk, 1), 114), (512,), 187, 99946, jnp.int32), jax.random.randint(jax.random.fold_in(jax.random.fold_in(_rk, 1), 115), (512,), 81, 99917, jnp.int32), jax.random.randint(jax.random.fold_in(jax.random.fold_in(_rk, 1), 116), (512,), 102, 99967, jnp.int32), jax.random.randint(jax.random.fold_in(jax.random.fold_in(_rk, 1), 117), (512,), 28, 99988, jnp.int32), jax.random.randint(jax.random.fold_in(jax.random.fold_in(_rk, 1), 118), (512,), 7, 99969, jnp.int32), jax.random.randint(jax.random.fold_in(jax.random.fold_in(_rk, 1), 119), (512,), 10, 12488, jnp.int32), jax.random.randint(jax.random.fold_in(jax.random.fold_in(_rk, 1), 120), (512,), 17, 99900, jnp.int32), jax.random.randint(jax.random.fold_in(jax.random.fold_in(_rk, 1), 121), (512,), 231, 99987, jnp.int32), jax.random.randint(jax.random.fold_in(jax.random.fold_in(_rk, 1), 122), (512,), 194, 99890, jnp.int32), jax.random.randint(jax.random.fold_in(jax.random.fold_in(_rk, 1), 123), (512,), 7, 12494, jnp.int32), jax.random.randint(jax.random.fold_in(jax.random.fold_in(_rk, 1), 124), (512,), 35, 99966, jnp.int32), jax.random.randint(jax.random.fold_in(jax.random.fold_in(_rk, 1), 125), (512,), 62, 99681, jnp.int32), jax.random.randint(jax.random.fold_in(jax.random.fold_in(_rk, 1), 126), (512,), 31, 99843, jnp.int32), jax.random.randint(jax.random.fold_in(jax.random.fold_in(_rk, 1), 127), (512,), 33, 99967, jnp.int32), jax.random.randint(jax.random.fold_in(jax.random.fold_in(_rk, 1), 128), (512,), 42, 99983, jnp.int32), jax.random.randint(jax.random.fold_in(jax.random.fold_in(_rk, 1), 129), (512,), 104, 99743, jnp.int32), jax.random.randint(jax.random.fold_in(jax.random.fold_in(_rk, 1), 130), (512,), 118, 99903, jnp.int32), jax.random.randint(jax.random.fold_in(jax.random.fold_in(_rk, 1), 131), (512,), 194, 99794, jnp.int32), jax.random.randint(jax.random.fold_in(jax.random.fold_in(_rk, 1), 132), (512,), 22, 99954, jnp.int32), jax.random.randint(jax.random.fold_in(jax.random.fold_in(_rk, 1), 133), (512,), 17, 99959, jnp.int32), jax.random.randint(jax.random.fold_in(jax.random.fold_in(_rk, 1), 134), (512,), 46, 99855, jnp.int32), jax.random.randint(jax.random.fold_in(jax.random.fold_in(_rk, 1), 135), (512,), 503, 99713, jnp.int32), jax.random.randint(jax.random.fold_in(jax.random.fold_in(_rk, 1), 136), (512,), 406, 99810, jnp.int32), jax.random.randint(jax.random.fold_in(jax.random.fold_in(_rk, 1), 137), (512,), 123, 12487, jnp.int32), jax.random.randint(jax.random.fold_in(jax.random.fold_in(_rk, 1), 138), (512,), 193, 99684, jnp.int32), jax.random.randint(jax.random.fold_in(jax.random.fold_in(_rk, 1), 139), (512,), 169, 99978, jnp.int32), jax.random.randint(jax.random.fold_in(jax.random.fold_in(_rk, 1), 140), (512,), 89, 99969, jnp.int32), jax.random.randint(jax.random.fold_in(jax.random.fold_in(_rk, 1), 141), (512,), 92, 99884, jnp.int32), jax.random.randint(jax.random.fold_in(jax.random.fold_in(_rk, 1), 142), (512,), 169, 99797, jnp.int32), jax.random.randint(jax.random.fold_in(jax.random.fold_in(_rk, 1), 143), (512,), 96, 12487, jnp.int32), jax.random.randint(jax.random.fold_in(jax.random.fold_in(_rk, 1), 144), (512,), 5, 99972, jnp.int32), jax.random.randint(jax.random.fold_in(jax.random.fold_in(_rk, 1), 145), (512,), 14, 99879, jnp.int32), jax.random.randint(jax.random.fold_in(jax.random.fold_in(_rk, 1), 146), (512,), 87, 99964, jnp.int32), jax.random.randint(jax.random.fold_in(jax.random.fold_in(_rk, 1), 147), (512,), 62, 99921, jnp.int32), jax.random.randint(jax.random.fold_in(jax.random.fold_in(_rk, 1), 148), (512,), 3, 99889, jnp.int32), jax.random.randint(jax.random.fold_in(jax.random.fold_in(_rk, 1), 149), (512,), 162, 99523, jnp.int32), jax.random.randint(jax.random.fold_in(jax.random.fold_in(_rk, 1), 150), (512,), 104, 99919, jnp.int32), jax.random.randint(jax.random.fold_in(jax.random.fold_in(_rk, 1), 151), (512,), 276, 99942, jnp.int32), jax.random.randint(jax.random.fold_in(jax.random.fold_in(_rk, 1), 152), (512,), 168, 99895, jnp.int32), jax.random.randint(jax.random.fold_in(jax.random.fold_in(_rk, 1), 153), (512,), 455, 99057, jnp.int32), jax.random.randint(jax.random.fold_in(jax.random.fold_in(_rk, 1), 154), (512,), 104, 99887, jnp.int32), jax.random.randint(jax.random.fold_in(jax.random.fold_in(_rk, 1), 155), (512,), 64, 99988, jnp.int32), jax.random.randint(jax.random.fold_in(jax.random.fold_in(_rk, 1), 156), (512,), 17, 99995, jnp.int32), jax.random.randint(jax.random.fold_in(jax.random.fold_in(_rk, 1), 157), (512,), 140, 99870, jnp.int32), jax.random.randint(jax.random.fold_in(jax.random.fold_in(_rk, 1), 158), (512,), 95, 99682, jnp.int32), jax.random.randint(jax.random.fold_in(jax.random.fold_in(_rk, 1), 159), (512,), 180, 99950, jnp.int32), jax.random.randint(jax.random.fold_in(jax.random.fold_in(_rk, 1), 160), (512,), 72, 12488, jnp.int32), jax.random.randint(jax.random.fold_in(jax.random.fold_in(_rk, 1), 161), (512,), 231, 12473, jnp.int32), jax.random.randint(jax.random.fold_in(jax.random.fold_in(_rk, 1), 162), (512,), 28, 12454, jnp.int32), jax.random.randint(jax.random.fold_in(jax.random.fold_in(_rk, 1), 163), (512,), 6, 99860, jnp.int32), jax.random.randint(jax.random.fold_in(jax.random.fold_in(_rk, 1), 164), (512,), 15, 99886, jnp.int32), jax.random.randint(jax.random.fold_in(jax.random.fold_in(_rk, 1), 165), (512,), 131, 99907, jnp.int32), jax.random.randint(jax.random.fold_in(jax.random.fold_in(_rk, 1), 166), (512,), 400, 99988, jnp.int32), jax.random.randint(jax.random.fold_in(jax.random.fold_in(_rk, 1), 167), (512,), 0, 99775, jnp.int32), jax.random.randint(jax.random.fold_in(jax.random.fold_in(_rk, 1), 168), (512,), 58, 99998, jnp.int32), jax.random.randint(jax.random.fold_in(jax.random.fold_in(_rk, 1), 169), (512,), 170, 99957, jnp.int32), jax.random.randint(jax.random.fold_in(jax.random.fold_in(_rk, 1), 170), (512,), 81, 99987, jnp.int32), jax.random.randint(jax.random.fold_in(jax.random.fold_in(_rk, 1), 171), (512,), 72, 99770, jnp.int32), jax.random.randint(jax.random.fold_in(jax.random.fold_in(_rk, 1), 172), (512,), 122, 99962, jnp.int32), jax.random.randint(jax.random.fold_in(jax.random.fold_in(_rk, 1), 173), (512,), 64, 99883, jnp.int32), jax.random.randint(jax.random.fold_in(jax.random.fold_in(_rk, 1), 174), (512,), 275, 99877, jnp.int32), jax.random.randint(jax.random.fold_in(jax.random.fold_in(_rk, 1), 175), (512,), 10, 99937, jnp.int32), jax.random.randint(jax.random.fold_in(jax.random.fold_in(_rk, 1), 176), (512,), 49, 99986, jnp.int32), jax.random.randint(jax.random.fold_in(jax.random.fold_in(_rk, 1), 177), (512,), 164, 99911, jnp.int32), jax.random.randint(jax.random.fold_in(jax.random.fold_in(_rk, 1), 178), (512,), 71, 12469, jnp.int32), jax.random.randint(jax.random.fold_in(jax.random.fold_in(_rk, 1), 179), (512,), 4, 99951, jnp.int32), jax.random.randint(jax.random.fold_in(jax.random.fold_in(_rk, 1), 180), (512,), 35, 99979, jnp.int32), jax.random.randint(jax.random.fold_in(jax.random.fold_in(_rk, 1), 181), (512,), 134, 99963, jnp.int32), jax.random.randint(jax.random.fold_in(jax.random.fold_in(_rk, 1), 182), (512,), 7, 99926, jnp.int32), jax.random.randint(jax.random.fold_in(jax.random.fold_in(_rk, 1), 183), (512,), 65, 99946, jnp.int32), jax.random.randint(jax.random.fold_in(jax.random.fold_in(_rk, 1), 184), (512,), 13, 99892, jnp.int32), jax.random.randint(jax.random.fold_in(jax.random.fold_in(_rk, 1), 185), (512,), 39, 99970, jnp.int32), jax.random.randint(jax.random.fold_in(jax.random.fold_in(_rk, 1), 186), (512,), 6, 99891, jnp.int32), jax.random.randint(jax.random.fold_in(jax.random.fold_in(_rk, 1), 187), (512,), 35, 12500, jnp.int32), jax.random.randint(jax.random.fold_in(jax.random.fold_in(_rk, 1), 188), (512,), 18, 99941, jnp.int32), jax.random.randint(jax.random.fold_in(jax.random.fold_in(_rk, 1), 189), (512,), 180, 99991, jnp.int32), jax.random.randint(jax.random.fold_in(jax.random.fold_in(_rk, 1), 190), (512,), 88, 99898, jnp.int32), jax.random.randint(jax.random.fold_in(jax.random.fold_in(_rk, 1), 191), (512,), 14, 12487, jnp.int32), jax.random.randint(jax.random.fold_in(jax.random.fold_in(_rk, 1), 192), (512,), 41, 12471, jnp.int32), jax.random.randint(jax.random.fold_in(jax.random.fold_in(_rk, 1), 193), (512,), 23, 99942, jnp.int32), jax.random.randint(jax.random.fold_in(jax.random.fold_in(_rk, 1), 194), (512,), 52, 99879, jnp.int32), jax.random.randint(jax.random.fold_in(jax.random.fold_in(_rk, 1), 195), (512,), 61, 99977, jnp.int32), jax.random.randint(jax.random.fold_in(jax.random.fold_in(_rk, 1), 196), (512,), 253, 99809, jnp.int32), jax.random.randint(jax.random.fold_in(jax.random.fold_in(_rk, 1), 197), (512,), 46, 99996, jnp.int32), jax.random.randint(jax.random.fold_in(jax.random.fold_in(_rk, 1), 198), (512,), 252, 99997, jnp.int32), jax.random.randint(jax.random.fold_in(jax.random.fold_in(_rk, 1), 199), (512,), 49, 99977, jnp.int32)], axis=1)
        return r_item_seq
    r_item_seq = _rec_inputs()

    def _L0_rec_setup():
        import jax, jax.numpy as jnp
        import numpy as np
        NUM_ITEMS = 12500
        EMBED_DIM = 128
        NUM_CLASSES = 100
        BATCH = 1024
        SEQ_LEN = 200

        def _masked_gru_last_state(item_seq, emb, W, U, b_i, b_r):
            D = W.shape[0]
            x = emb[item_seq]
            mask = item_seq != 0
            xs = jnp.swapaxes(x, 0, 1)
            ms = jnp.swapaxes(mask, 0, 1)
            h0 = jnp.zeros((item_seq.shape[0], D), dtype=x.dtype)

            def step(h, inp):
                x_t, m_t = inp
                mx = x_t @ W + b_i
                mh = h @ U + b_r
                z = jax.nn.sigmoid(mx[:, :D] + mh[:, :D])
                r = jax.nn.sigmoid(mx[:, D:2 * D] + mh[:, D:2 * D])
                hh = jnp.tanh(mx[:, 2 * D:] + r * mh[:, 2 * D:])
                h_new = z * h + (1.0 - z) * hh
                h = jnp.where(m_t[:, None], h_new, h)
                return (h, None)
            h_last, _ = jax.lax.scan(step, h0, (xs, ms))
            return h_last
        key = jax.random.key(seed)
        ks = jax.random.split(key, 8)
        D = EMBED_DIM
        item_seq = jax.random.randint(ks[0], (BATCH, SEQ_LEN), 0, NUM_ITEMS, dtype=jnp.int32)
        scale = 1.0 / np.sqrt(D)
        emb = jax.random.normal(ks[1], (NUM_ITEMS, D), dtype=jnp.float32) * 0.05
        W = jax.random.normal(ks[2], (D, 3 * D), dtype=jnp.float32) * scale
        U = jax.random.normal(ks[3], (D, 3 * D), dtype=jnp.float32) * scale
        b_i = jax.random.normal(ks[4], (3 * D,), dtype=jnp.float32) * 0.01
        b_r = jax.random.normal(ks[5], (3 * D,), dtype=jnp.float32) * 0.01
        Wout = jax.random.normal(ks[6], (D, NUM_CLASSES), dtype=jnp.float32) * scale
        bout = jnp.zeros((NUM_CLASSES,), dtype=jnp.float32)
        return {'item_seq': item_seq, 'emb': emb, 'W': W, 'U': U, 'b_i': b_i, 'b_r': b_r, 'Wout': Wout, 'bout': bout}
    _L0_rec_all = _L0_rec_setup()
    _L0_rec_in = {k: v for k, v in _L0_rec_all.items() if k in ('emb', 'W', 'U', 'b_i', 'b_r', 'Wout', 'bout')}
    del _L0_rec_all
    return {'r_item_seq': r_item_seq, 'L0_rec_emb': _L0_rec_in['emb'], 'L0_rec_W': _L0_rec_in['W'], 'L0_rec_U': _L0_rec_in['U'], 'L0_rec_b_i': _L0_rec_in['b_i'], 'L0_rec_b_r': _L0_rec_in['b_r'], 'L0_rec_Wout': _L0_rec_in['Wout'], 'L0_rec_bout': _L0_rec_in['bout']}

def reference(r_item_seq, L0_rec_emb, L0_rec_W, L0_rec_U, L0_rec_b_i, L0_rec_b_r, L0_rec_Wout, L0_rec_bout):
    import jax
    import jax.numpy as jnp

    def _L0_rec_ref(item_seq, emb, W, U, b_i, b_r, Wout, bout):
        import jax, jax.numpy as jnp
        import numpy as np
        NUM_ITEMS = 12500
        EMBED_DIM = 128
        NUM_CLASSES = 100
        BATCH = 1024
        SEQ_LEN = 200

        def _masked_gru_last_state(item_seq, emb, W, U, b_i, b_r):
            D = W.shape[0]
            x = emb[item_seq]
            mask = item_seq != 0
            xs = jnp.swapaxes(x, 0, 1)
            ms = jnp.swapaxes(mask, 0, 1)
            h0 = jnp.zeros((item_seq.shape[0], D), dtype=x.dtype)

            def step(h, inp):
                x_t, m_t = inp
                mx = x_t @ W + b_i
                mh = h @ U + b_r
                z = jax.nn.sigmoid(mx[:, :D] + mh[:, :D])
                r = jax.nn.sigmoid(mx[:, D:2 * D] + mh[:, D:2 * D])
                hh = jnp.tanh(mx[:, 2 * D:] + r * mh[:, 2 * D:])
                h_new = z * h + (1.0 - z) * hh
                h = jnp.where(m_t[:, None], h_new, h)
                return (h, None)
            h_last, _ = jax.lax.scan(step, h0, (xs, ms))
            return h_last
        h_last = _masked_gru_last_state(item_seq, emb, W, U, b_i, b_r)
        logits = h_last @ Wout + bout
        return jax.nn.softmax(logits, axis=-1)
    y = _L0_rec_ref(r_item_seq, L0_rec_emb, L0_rec_W, L0_rec_U, L0_rec_b_i, L0_rec_b_r, L0_rec_Wout, L0_rec_bout)
    return y

_drawn_inputs = setup_inputs


def setup_inputs(seed=0):
    import zlib

    import numpy as np

    out = dict(_drawn_inputs(seed))
    spreads = {'L0_rec_bout': (0.0, 0.1)}
    factors = {'L0_rec_b_i': 5.587, 'L0_rec_b_r': 8.0}
    for name, (base, spread) in spreads.items():
        noise = np.random.default_rng([zlib.crc32(name.encode()), seed]).standard_normal(out[name].shape)
        drawn = base * np.exp(spread * noise) if base else spread * noise
        out[name] = jnp.asarray(drawn.astype(out[name].dtype))
    for name, factor in factors.items():
        out[name] = (out[name] * factor).astype(out[name].dtype)
    return out
```

```python
from contextlib import ExitStack

import concourse.bass as bass
from concourse import mybir

F32 = mybir.dt.float32
BF16 = mybir.dt.bfloat16
I32 = mybir.dt.int32
ALU = mybir.AluOpType
ACT = mybir.ActivationFunctionType
AX = mybir.AxisListType

P = 128
BLOCKS = 4
CHAINS = 2
PER = BLOCKS // CHAINS
RING = 20
HALF = RING // 2
GROUP = 4
PINNED = 1.0e30


def gru(nc: bass.Bass, item_seq, emb, W, U, b_i, b_r, Wout, bout, out):
    BATCH, STEPS = item_seq.shape
    ITEMS, D = emb.shape
    GATES = W.shape[1]
    CLASSES = Wout.shape[1]
    COLS = PER * P
    assert D == P and GATES == 3 * D and BATCH == BLOCKS * P and STEPS % RING == 0
    TURNS = STEPS // RING
    TILES = ITEMS // P
    REST = ITEMS - TILES * P
    GROUPS = TILES // GROUP
    assert TILES == GROUPS * GROUP + 1 and 0 < REST < P and GROUPS % 2 == 0

    table = nc.dram_tensor("table", [ITEMS + 1, GATES], F32, kind="Internal").ap()
    table_tiles = table[0:TILES * P, :].rearrange("(p j) n -> p j n", j=TILES)
    emb_tiles = emb[0:TILES * P, :].rearrange("(p j) d -> p j d", j=TILES)

    with ExitStack() as ctx:
        def sb(name, shape, dt=F32):
            return ctx.enter_context(nc.sbuf_tensor(name, shape, dt))

        def sem(name):
            return ctx.enter_context(nc.semaphore(name))

        def per_chain(name):
            return [sem(f"{name}{c}") for c in range(CHAINS)]

        raw = sb("raw", [P, RING, BLOCKS, D])
        ring = sb("ring", [P, RING, BLOCKS, GATES])
        emb_in = [ring[:, q, :, :].rearrange("p a b -> p (a b)")[:, 0:GROUP * D] for q in range(2)]
        emb_t = [ring[:, 2 + q, :, :].rearrange("p a b -> p (a b)")[:, 0:GROUP * D] for q in range(2)]
        proj = [ring[:, 4 + q, :, :] for q in range(2)]

        seq = sb("seq", [P, BLOCKS, STEPS], I32)
        row_f = sb("row_f", [P, BLOCKS, STEPS])
        pad_f = sb("pad_f", [P, BLOCKS, STEPS])
        row_raw = sb("row_raw", [P, RING, BLOCKS], I32)
        row_table = sb("row_table", [P, STEPS, BLOCKS], I32)
        row_now = sb("row_now", [P, 2, HALF * BLOCKS], I32)
        pin = sb("pin", [P, RING, BLOCKS], BF16)
        pad_row = sb("pad_row", [1, GATES])
        ident = sb("ident", [P, P])
        ident_bf = sb("ident_bf", [P, P], BF16)
        W_sb = sb("W_sb", [P, GATES])
        U_sb = sb("U_sb", [P, GATES])
        Wout_sb = sb("Wout_sb", [P, CLASSES])
        bout_sb = sb("bout_sb", [P, CLASSES])
        bi = sb("bi", [P, 3])
        br = sb("br", [P, 3])
        b_gates = sb("b_gates", [P, 2])
        b_keep = sb("b_keep", [P, 1])
        h = [sb(f"h{c}", [P, COLS]) for c in range(CHAINS)]
        x_t = [sb(f"x_t{c}", [P, COLS]) for c in range(CHAINS)]
        r = [sb(f"r{c}", [P, COLS]) for c in range(CHAINS)]
        z = [sb(f"z{c}", [P, COLS]) for c in range(CHAINS)]
        one_z = [sb(f"one_z{c}", [P, COLS]) for c in range(CHAINS)]
        rh = [sb(f"rh{c}", [P, COLS]) for c in range(CHAINS)]
        pre = [sb(f"pre{c}", [P, COLS]) for c in range(CHAINS)]
        cand = [sb(f"cand{c}", [P, COLS]) for c in range(CHAINS)]
        zh = [sb(f"zh{c}", [P, COLS]) for c in range(CHAINS)]
        zc = [sb(f"zc{c}", [P, COLS]) for c in range(CHAINS)]
        logits = sb("logits", [P, BLOCKS, CLASSES])
        probs = sb("probs", [P, BLOCKS, CLASSES])
        top = sb("top", [P, BLOCKS])
        neg_top = sb("neg_top", [P, BLOCKS])
        total = sb("total", [P, BLOCKS])
        inv_total = sb("inv_total", [P, BLOCKS])

        bank = [ctx.enter_context(nc.psum_tensor(f"bank{i}", [P, 512], F32)) for i in range(8)]
        gate_bank = [[bank[6], bank[2]], [bank[0], bank[4]]]
        cand_bank = [[bank[7], bank[3]], [bank[1], bank[5]]]
        x_bank = bank[0:2]
        emb_bank = bank[0:2]
        proj_bank = bank[2:6]
        ODD = 1

        s_seq = sem("seq_loaded")
        s_w = sem("weights_loaded")
        s_const = sem("constants_ready")
        s_ident0 = sem("ident_zeroed")
        s_ident = sem("ident_ready")
        s_idx = sem("index_steps")
        s_raw_rows = sem("raw_rows_ready")
        s_table_rows = sem("table_rows_ready")
        s_bias = sem("biases_ready")
        s_emb = [sem(f"emb_loaded{q}") for q in range(2)]
        s_embt = sem("emb_transposed")
        s_embc = sem("emb_t_copied")
        s_proj = sem("projected")
        s_pact = sem("proj_copied_scalar")
        s_pdve = sem("proj_copied_vector")
        s_store = [sem(f"table_stored{q}") for q in range(2)]
        s_padrow = sem("pad_row_stored")
        s_now = [sem(f"rows_staged{q}") for q in range(2)]
        s_slot = [per_chain(f"slot{s}_gathered") for s in range(RING)]
        s_free = per_chain("slots_free")
        s_paced = sem("gathers_paced")
        s_xt = per_chain("x_transposed")
        s_xc = per_chain("x_t_copied")
        s_gates = per_chain("gates_summed")
        s_cand = per_chain("cand_summed")
        s_r = per_chain("r_ready")
        s_z = per_chain("z_ready")
        s_zz = per_chain("one_z_ready")
        s_rh = per_chain("rh_ready")
        s_pre = per_chain("pre_ready")
        s_tanh = per_chain("cand_ready")
        s_zc = per_chain("zc_ready")
        s_h = per_chain("h_ready")
        s_logit_ps = sem("logits_summed")
        s_logit = sem("logits_ready")
        s_top = sem("top_ready")
        s_ntop = sem("neg_top_ready")
        s_exp = sem("exp_ready")
        s_inv = sem("inv_ready")
        s_prob = sem("probs_ready")
        s_out = sem("out_stored")

        block = ctx.enter_context(nc.Block())

        def over_groups(eng, pair):
            pair(0)
            with eng.Fori(1, GROUPS // 2 - 1) as two:
                pair(two * 2)
            pair(GROUPS - 2)

        @block.sync
        def _(sp):
            sp.dma_start(seq[:, :, :], item_seq.rearrange("(k p) t -> p k t", p=P)).then_inc(s_seq, 16)

            def load_emb(g, q):
                sp.dma_start(emb_in[q].rearrange("p (j d) -> p j d", d=D),
                             emb_tiles[:, bass.ds(g * GROUP, GROUP), :]).then_inc(s_emb[q], 16)

            load_emb(0, 0)
            sp.dma_start(W_sb[:, :], W).then_inc(s_w, 16)
            load_emb(1, 1)
            sp.dma_start(U_sb[:, :], U).then_inc(s_w, 16)
            sp.dma_start(bi[:, :], b_i).then_inc(s_w, 16)
            sp.dma_start(br[:, :], b_r).then_inc(s_w, 16)
            sp.dma_start(Wout_sb[:, :], Wout).then_inc(s_w, 16)
            sp.dma_start(bout_sb[:, :], bout.partition_broadcast(P)).then_inc(s_w, 16)
            sp.wait_ge(s_const, 1)
            sp.dma_start(table[ITEMS:ITEMS + 1, :], pad_row[:, :]).then_inc(s_padrow, 16)

            def store(g, q):
                sp.wait_ge(s_pact, (g + 1) * (GROUP // 2))
                sp.wait_ge(s_pdve, (g + 1) * (GROUP // 2))
                sp.dma_start(table_tiles[:, bass.ds(g * GROUP, GROUP), :], proj[q]).then_inc(s_store[q], 16)

            def pair(g):
                for q in range(2):
                    sp.wait_ge(s_embt, g + q + 1)
                    if not isinstance(g, int) or g + q + 2 < GROUPS:
                        load_emb(g + q + 2, q)
                    elif g + q + 2 == GROUPS:
                        sp.dma_start(emb_in[0][:, 0:D], emb_tiles[:, TILES - 1, :]).then_inc(s_emb[0], 16)
                        sp.dma_start(emb_in[0][0:REST, D:2 * D], emb[TILES * P:ITEMS, :]).then_inc(s_emb[0], 16)
                    store(g + q, q)

            over_groups(sp, pair)
            sp.wait_ge(s_pact, GROUPS * (GROUP // 2) + 1)
            sp.dma_start(table_tiles[:, TILES - 1, :], proj[0][:, 0, :]).then_inc(s_store[0], 16)
            sp.wait_ge(s_pdve, GROUPS * (GROUP // 2) + 1)
            sp.dma_start(table[TILES * P:ITEMS, :], proj[0][0:REST, 1, :]).then_inc(s_store[0], 16)

            def stage_rows(turn, q):
                sp.dma_start(row_now[:, q, :],
                             row_table[:, :, :].rearrange("p t k -> p (t k)")[
                                 :, bass.ds((turn * RING + q * HALF) * BLOCKS, HALF * BLOCKS)]
                             ).then_inc(s_now[q], 16)

            sp.wait_ge(s_table_rows, 1)
            stage_rows(1, 0)
            stage_rows(1, 1)
            with sp.Fori(2, TURNS) as turn:
                for q in range(2):
                    for s in range(q * HALF, (q + 1) * HALF):
                        for c in range(CHAINS):
                            sp.wait_ge(s_slot[s][c], turn * (16 * PER))
                    stage_rows(turn, q)

            sp.wait_ge(s_prob, BLOCKS)
            sp.dma_start(out.rearrange("(k p) n -> p k n", p=P), probs[:, :, :]).then_inc(s_out, 16)
            sp.wait_ge(s_out, 16)

        @block.gpsimd
        def _(pool):
            pool.memset(ident[:, :], 0.0).then_inc(s_ident0, 1)
            pool.wait_ge(s_ident0, 1)
            pool.affine_select(out=ident[:, :], in_=ident[:, :], compare_op=ALU.not_equal, fill=1.0,
                               base=0, pattern=[[-1, P]], channel_multiplier=1).then_inc(s_ident, 1)

            def gather(s, k, dst, src, rows):
                pool.indirect_dma_start(dst, None, src, bass.IndirectOffsetOnAxis(rows, 0)
                                        ).then_inc(s_slot[s][k // PER], 16)

            pool.wait_ge(s_raw_rows, 1)
            for s in range(RING):
                for k in range(BLOCKS):
                    gather(s, k, raw[:, s, k, :], emb, row_raw[:, s, k:k + 1])

            pool.wait_ge(s_store[0], 16 * (GROUPS // 2 + 2))
            pool.wait_ge(s_store[1], 16 * (GROUPS // 2))
            pool.wait_ge(s_padrow, 16)
            for s in range(RING):
                for c in range(CHAINS):
                    pool.wait_ge(s_slot[s][c], 16 * PER)
            with pool.Fori(1, TURNS) as turn:
                for s in range(RING):
                    if s % HALF == 0:
                        pool.wait_ge(s_now[s // HALF], turn * 16)
                    for c in range(CHAINS):
                        pool.wait_ge(s_free[c], (turn - 1) * RING + s + 1)
                        pool.sem_inc(s_paced, 1)
                        for k in range(c * PER, (c + 1) * PER):
                            i = (s % HALF) * BLOCKS + k
                            gather(s, k, ring[:, s, k, :], table, row_now[:, s // HALF, i:i + 1])

        @block.tensor
        def _(pe):
            def transpose_group(g, q, tiles=GROUP):
                if tiles == GROUP:
                    pe.wait_ge(s_emb[q], (g - q) * 8 + 16)
                else:
                    pe.wait_ge(s_emb[q], 16 * (GROUPS // 2 + 2))
                if not isinstance(g, int) or g >= 2:
                    pe.wait_ge(s_embc, g - 1)
                for j in range(tiles):
                    n = P if tiles == GROUP or j == 0 else REST
                    last = pe.matmul(emb_bank[q][:, j * P:j * P + n], emb_in[q][0:n, j * D:(j + 1) * D],
                                     ident[0:n, 0:n], start=(j == 0), stop=True, is_transpose=True,
                                     skip_group_check=True)
                last.then_inc(s_embt, 1)

            def project_group(g, q, tiles=GROUP):
                pe.wait_ge(s_embc, g + 1)
                for j in range(tiles):
                    n = P if tiles == GROUP or j == 0 else REST
                    if not isinstance(g, int) or g >= 1:
                        pe.wait_ge((s_pact, s_pdve)[j % 2], (g - 1) * (GROUP // 2) + j // 2 + 1)
                    pe.matmul(proj_bank[j][0:n, 0:GATES], emb_t[q][:, j * P:j * P + n], W_sb[:, :],
                              start=True, stop=True).then_inc(s_proj, 1)

            pe.wait_ge(s_ident, 1)
            transpose_group(0, 0)
            pe.wait_ge(s_w, 16 * 6)

            def pair(g):
                for q in range(2):
                    if isinstance(g, int) and g + q + 1 == GROUPS:
                        transpose_group(GROUPS, 0, 2)
                    else:
                        transpose_group(g + q + 1, 1 - q)
                    project_group(g + q, q)

            over_groups(pe, pair)
            project_group(GROUPS, 0, 2)

            def transpose_x(t, c):
                pe.wait_ge(s_slot[t][c], 16 * PER)
                for b in range(PER):
                    last = pe.matmul(x_bank[c][:, b * P:(b + 1) * P], raw[:, t, c * PER + b, :],
                                     ident[:, :], start=(b == 0), stop=True, is_transpose=True,
                                     skip_group_check=True)
                last.then_inc(s_xt[c], 1)

            def project_x(t, c):
                gates, cands = gate_bank[c][ODD], cand_bank[c][ODD]
                pe.wait_ge(s_xc[c], t + 1)
                if t > 0:
                    pe.wait_ge(s_zz[c], t)
                    pe.wait_ge(s_pre[c], t)
                pe.matmul(gates[:, 0:COLS], W_sb[:, D:2 * D], x_t[c][:, :], start=True, stop=False,
                          skip_group_check=True)
                pe.matmul(gates[:, COLS:2 * COLS], W_sb[:, 0:D], x_t[c][:, :], start=False, stop=False,
                          skip_group_check=True)
                for b in range(PER):
                    k = c * PER + b
                    pe.matmul(gates[:, COLS + b * P:COLS + (b + 1) * P],
                              pin[:, t, k:k + 1].broadcast_to([P, P]), ident_bf[:, :],
                              start=False, stop=False, skip_group_check=True)
                pe.matmul(cands[:, COLS:2 * COLS], W_sb[:, 2 * D:3 * D], x_t[c][:, :], start=True,
                          stop=False, skip_group_check=True)

            def transpose_rows(turn, s, c):
                gates, cands = gate_bank[c][s % 2], cand_bank[c][s % 2]
                pe.wait_ge(s_slot[s][c], (turn + 1) * (16 * PER))
                for b in range(PER):
                    k = c * PER + b
                    for dst, col, g, start in ((gates, 0, 1, b == 0), (gates, COLS, 0, False),
                                               (cands, COLS, 2, b == 0)):
                        last = pe.matmul(dst[:, col + b * P:col + (b + 1) * P],
                                         ring[:, s, k, g * D:(g + 1) * D], ident[:, :],
                                         start=start, stop=False, is_transpose=True,
                                         skip_group_check=True)
                last.then_inc(s_free[c], 1)

            def recur(t, parity, c):
                gates, cands = gate_bank[c][parity], cand_bank[c][parity]
                pe.wait_ge(s_h[c], t + 1)
                pe.matmul(gates[:, 0:COLS], U_sb[:, D:2 * D], h[c][:, :], start=False, stop=True,
                          skip_group_check=True)
                pe.matmul(gates[:, COLS:2 * COLS], U_sb[:, 0:D], h[c][:, :], start=False, stop=True,
                          skip_group_check=True).then_inc(s_gates[c], 1)
                pe.matmul(cands[:, 0:COLS], U_sb[:, 2 * D:3 * D], h[c][:, :], start=False, stop=True,
                          skip_group_check=True).then_inc(s_cand[c], 1)

            pe.wait_ge(s_pact, GROUPS * (GROUP // 2) + 1)
            pe.wait_ge(s_pdve, GROUPS * (GROUP // 2) + 1)
            pe.wait_ge(s_bias, 1)
            for c in range(CHAINS):
                transpose_x(0, c)
            for t in range(RING):
                for c in range(CHAINS):
                    project_x(t, c)
                    recur(t, ODD, c)
                    if t + 1 < RING:
                        transpose_x(t + 1, c)

            with pe.Fori(1, TURNS) as turn:
                for s in range(RING):
                    for c in range(CHAINS):
                        transpose_rows(turn, s, c)
                        recur(turn * RING + s, s % 2, c)

            for k in range(BLOCKS):
                c, b = k // PER, k % PER
                if b == 0:
                    pe.wait_ge(s_h[c], STEPS + 1)
                last = pe.matmul(gate_bank[0][0][:, k * CLASSES:(k + 1) * CLASSES], h[c][:, b * P:(b + 1) * P],
                                 Wout_sb[:, :], start=(k == 0), stop=True, skip_group_check=True)
            last.then_inc(s_logit_ps, 1)

        @block.scalar
        def _(act):
            def copy_proj(g, q, j):
                act.wait_ge(s_proj, g * GROUP + j + 1)
                if not isinstance(g, int) or g >= 2:
                    act.wait_ge(s_store[q], (g - q) * 8)
                act.copy(proj[q][:, j, :], proj_bank[j][:, 0:GATES]).then_inc(s_pact, 1)

            def pair(g):
                for q in range(2):
                    for j in range(0, GROUP, 2):
                        copy_proj(g + q, q, j)

            over_groups(act, pair)
            copy_proj(GROUPS, 0, 0)

            def copy_x(t, c):
                act.wait_ge(s_xt[c], t + 1)
                act.copy(x_t[c][:, :], x_bank[c][:, 0:COLS]).then_inc(s_xc[c], 1)

            def gates(t, parity, c):
                act.wait_ge(s_gates[c], t + 1)
                act.activation(r[c][:, :], gate_bank[c][parity][:, 0:COLS], ACT.Sigmoid,
                               bias=b_gates[:, 1:2]).then_inc(s_r[c], 1)
                act.activation(z[c][:, :], gate_bank[c][parity][:, COLS:2 * COLS], ACT.Sigmoid,
                               bias=b_gates[:, 0:1]).then_inc(s_z[c], 1)
                act.activation(one_z[c][:, :], gate_bank[c][parity][:, COLS:2 * COLS], ACT.Sigmoid,
                               bias=b_keep[:, 0:1], scale=-1.0).then_inc(s_zz[c], 1)

            def candidate(t, c):
                act.wait_ge(s_pre[c], t + 1)
                act.activation(cand[c][:, :], pre[c][:, :], ACT.Tanh, bias=bi[:, 2:3]).then_inc(s_tanh[c], 1)

            act.wait_ge(s_bias, 1)
            for c in range(CHAINS):
                copy_x(0, c)
            for t in range(RING):
                for c in range(CHAINS):
                    gates(t, ODD, c)
                    if t + 1 < RING:
                        copy_x(t + 1, c)
                    candidate(t, c)
            with act.Fori(1, TURNS) as turn:
                for s in range(RING):
                    for c in range(CHAINS):
                        gates(turn * RING + s, s % 2, c)
                        candidate(turn * RING + s, c)

            act.wait_ge(s_ntop, 1)
            for k in range(BLOCKS):
                act.activation(probs[:, k, :], logits[:, k, :], ACT.Exp, bias=neg_top[:, k:k + 1],
                               accum_out=total[:, k:k + 1]).then_inc(s_exp, 1)

        @block.vector
        def _(dve):
            dve.memset(pad_row[:, :], 0.0).then_inc(s_idx, 1)
            for c in range(CHAINS):
                dve.memset(h[c][:, :], 0.0).then_inc(s_h[c], 1)
                dve.sem_inc(s_free[c], RING)
            dve.wait_ge(s_idx, 1)
            dve.memset(pad_row[:, 0:D], PINNED).then_inc(s_const, 1)

            dve.wait_ge(s_seq, 16)
            dve.tensor_scalar(row_f[:, :, :], seq[:, :, :], 0.0, float(ITEMS), ALU.is_lt, ALU.mult).then_inc(s_idx, 1)
            dve.wait_ge(s_idx, 2)
            dve.tensor_tensor(row_f[:, :, :], row_f[:, :, :], seq[:, :, :], ALU.add).then_inc(s_idx, 1)
            dve.wait_ge(s_idx, 3)
            dve.tensor_scalar(row_f[:, :, :], row_f[:, :, :], 0.0, float(ITEMS - 1), ALU.max, ALU.min).then_inc(s_idx, 1)
            dve.wait_ge(s_idx, 4)
            dve.tensor_copy(row_raw[:, :, :], row_f[:, :, 0:RING].rearrange("p k t -> p t k")).then_inc(s_raw_rows, 1)
            dve.tensor_scalar(pad_f[:, :, :], seq[:, :, :], 0.0, float(ITEMS), ALU.is_equal, ALU.mult).then_inc(s_idx, 1)
            dve.wait_ge(s_idx, 5)
            dve.tensor_tensor(row_table[:, :, :], row_f[:, :, :].rearrange("p k t -> p t k"),
                              pad_f[:, :, :].rearrange("p k t -> p t k"), ALU.add).then_inc(s_table_rows, 1)
            dve.tensor_scalar(pin[:, :, :], pad_f[:, :, 0:RING].rearrange("p k t -> p t k"), PINNED / ITEMS,
                              None, ALU.mult)
            dve.wait_ge(s_w, 16 * 6)
            dve.tensor_tensor(b_gates[:, :], bi[:, 0:2], br[:, 0:2], ALU.add).then_inc(s_idx, 1)
            dve.wait_ge(s_idx, 6)
            dve.tensor_scalar(b_keep[:, :], b_gates[:, 0:1], -1.0, None, ALU.mult)
            dve.wait_ge(s_ident, 1)
            dve.tensor_copy(ident_bf[:, :], ident[:, :]).then_inc(s_bias, 1)

            def copy_emb(g, q, tiles=GROUP):
                dve.wait_ge(s_embt, g + 1)
                if not isinstance(g, int) or g >= 2:
                    dve.wait_ge(s_proj, (g - 1) * GROUP)
                dve.tensor_copy(emb_t[q][:, 0:tiles * P], emb_bank[q][:, 0:tiles * P]).then_inc(s_embc, 1)

            def copy_proj(g, q, j, n=P):
                dve.wait_ge(s_proj, g * GROUP + j + 1)
                if not isinstance(g, int) or g >= 2:
                    dve.wait_ge(s_store[q], (g - q) * 8)
                dve.tensor_copy(proj[q][0:n, j, :], proj_bank[j][0:n, 0:GATES]).then_inc(s_pdve, 1)

            copy_emb(0, 0)

            def pair(g):
                for q in range(2):
                    if isinstance(g, int) and g + q + 1 == GROUPS:
                        dve.wait_ge(s_embt, GROUPS + 1)
                        dve.wait_ge(s_proj, (GROUPS - 1) * GROUP)
                        dve.tensor_copy(emb_t[0][:, 0:P + REST], emb_bank[0][:, 0:P + REST]).then_inc(s_embc, 1)
                    else:
                        copy_emb(g + q + 1, 1 - q)
                    for j in range(1, GROUP, 2):
                        copy_proj(g + q, q, j)

            over_groups(dve, pair)
            copy_proj(GROUPS, 0, 1, REST)
            def reset_h(t, parity, c):
                dve.wait_ge(s_cand[c], t + 1)
                dve.wait_ge(s_r[c], t + 1)
                dve.scalar_tensor_tensor(out=rh[c][:, :], in0=cand_bank[c][parity][:, 0:COLS],
                                         scalar=br[:, 2:3], in1=r[c][:, :], op0=ALU.add,
                                         op1=ALU.mult).then_inc(s_rh[c], 1)
                dve.wait_ge(s_rh[c], t + 1)
                dve.tensor_tensor(pre[c][:, :], rh[c][:, :], cand_bank[c][parity][:, COLS:2 * COLS],
                                  ALU.add).then_inc(s_pre[c], 1)

            def update(t, c):
                dve.wait_ge(s_z[c], t + 1)
                dve.tensor_tensor(zh[c][:, :], z[c][:, :], h[c][:, :], ALU.mult)
                dve.wait_ge(s_tanh[c], t + 1)
                dve.tensor_tensor(zc[c][:, :], one_z[c][:, :], cand[c][:, :], ALU.mult).then_inc(s_zc[c], 1)
                dve.wait_ge(s_zc[c], t + 1)
                dve.tensor_tensor(h[c][:, :], zh[c][:, :], zc[c][:, :], ALU.add).then_inc(s_h[c], 1)

            for t in range(RING):
                for c in range(CHAINS):
                    reset_h(t, ODD, c)
                    update(t, c)
            with dve.Fori(1, TURNS) as turn:
                for s in range(RING):
                    for c in range(CHAINS):
                        reset_h(turn * RING + s, s % 2, c)
                        update(turn * RING + s, c)

            dve.wait_ge(s_logit_ps, 1)
            for k in range(BLOCKS):
                dve.tensor_tensor(logits[:, k, :], gate_bank[0][0][:, k * CLASSES:(k + 1) * CLASSES],
                                  bout_sb[:, :], ALU.add).then_inc(s_logit, 1)
            dve.wait_ge(s_logit, BLOCKS)
            dve.tensor_reduce(top[:, :], logits[:, :, :], AX.X, ALU.max).then_inc(s_top, 1)
            dve.wait_ge(s_top, 1)
            dve.tensor_scalar(neg_top[:, :], top[:, :], -1.0, None, ALU.mult).then_inc(s_ntop, 1)
            dve.wait_ge(s_exp, BLOCKS)
            dve.reciprocal(inv_total[:, :], total[:, :]).then_inc(s_inv, 1)
            dve.wait_ge(s_inv, 1)
            for k in range(BLOCKS):
                dve.tensor_scalar(probs[:, k, :], probs[:, k, :], inv_total[:, k:k + 1], None,
                                  ALU.mult).then_inc(s_prob, 1)


_INS = ["r_item_seq", "L0_rec_emb", "L0_rec_W", "L0_rec_U", "L0_rec_b_i", "L0_rec_b_r", "L0_rec_Wout", "L0_rec_bout"]


def kernel(**inputs):
    import numpy as np
    import concourse.bacc as bacc
    from concourse.bass_utils import run_bass_kernel_spmd as run

    nc = bacc.Bacc("TRN2", target_bir_lowering=False, num_devices=1)
    arrays, args = {}, []
    for name in _INS:
        a = np.asarray(inputs[name])
        if name in ("L0_rec_b_i", "L0_rec_b_r"):
            a = a.reshape(3, -1).T
        a = np.ascontiguousarray(a)
        arrays[f"in_{name}"] = a
        args.append(nc.dram_tensor(f"in_{name}", a.shape, mybir.dt.from_np(a.dtype), kind="ExternalInput").ap())
    shape = (inputs["r_item_seq"].shape[0], inputs["L0_rec_Wout"].shape[1])
    out = nc.dram_tensor("out_probs", shape, F32, kind="ExternalOutput").ap()
    gru(nc, *args, out)
    return run(nc, [arrays], core_ids=[0]).results[0]["out_probs"]
```

```python
from contextlib import ExitStack

import concourse.bass as bass
from concourse import mybir

F32 = mybir.dt.float32
I32 = mybir.dt.int32
ALU = mybir.AluOpType
ACT = mybir.ActivationFunctionType
AX = mybir.AxisListType

P = 128
BLOCKS = 4
CHAINS = 2
PER = BLOCKS // CHAINS
RING = 8
HALF = RING // 2
GROUP = 4
AHEAD = 4
PINNED = 1.0e30


def gru(nc: bass.Bass, item_seq, emb, W, U, b_i, b_r, Wout, bout, out):
    BATCH, STEPS = item_seq.shape
    ITEMS, D = emb.shape
    GATES = W.shape[1]
    CLASSES = Wout.shape[1]
    COLS = PER * P
    assert D == P and GATES == 3 * D and BATCH == BLOCKS * P and STEPS % RING == 0
    TURNS = STEPS // RING
    TILES = ITEMS // P
    REST = ITEMS - TILES * P
    GROUPS = TILES // GROUP
    assert TILES == GROUPS * GROUP + 1 and 0 < REST < P and GROUPS % AHEAD == 0

    table = nc.dram_tensor("table", [ITEMS + 1, GATES], F32, kind="Internal").ap()
    table_tiles = table[0:TILES * P, :].rearrange("(p j) n -> p j n", j=TILES)
    emb_tiles = emb[0:TILES * P, :].rearrange("(p j) d -> p j d", j=TILES)

    with ExitStack() as ctx:
        def sb(name, shape, dt=F32):
            return ctx.enter_context(nc.sbuf_tensor(name, shape, dt))

        def sem(name):
            return ctx.enter_context(nc.semaphore(name))

        def per_chain(name):
            return [sem(f"{name}{c}") for c in range(CHAINS)]

        emb_in = [sb(f"emb_in{q}", [P, GROUP * D]) for q in range(AHEAD)]
        emb_t = [sb(f"emb_t{p}", [P, GROUP * D]) for p in range(2)]
        proj = [sb(f"proj{p}", [P, GROUP, GATES]) for p in range(2)]
        ring = sb("ring", [P, RING, BLOCKS, GATES])

        seq = sb("seq", [P, BLOCKS, STEPS], I32)
        row_f = sb("row_f", [P, BLOCKS, STEPS])
        pad_f = sb("pad_f", [P, BLOCKS, STEPS])
        row_table = sb("row_table", [P, STEPS, BLOCKS], I32)
        row_now = sb("row_now", [P, 2, HALF * BLOCKS], I32)
        pad_row = sb("pad_row", [1, GATES])
        ident = sb("ident", [P, P])
        W_sb = sb("W_sb", [P, GATES])
        U_sb = sb("U_sb", [P, GATES])
        Wout_sb = sb("Wout_sb", [P, CLASSES])
        bout_sb = sb("bout_sb", [P, CLASSES])
        bi = sb("bi", [P, 3])
        br = sb("br", [P, 3])
        b_gates = sb("b_gates", [P, 2])
        b_keep = sb("b_keep", [P, 1])
        h = [sb(f"h{c}", [P, COLS]) for c in range(CHAINS)]
        r = [sb(f"r{c}", [P, COLS]) for c in range(CHAINS)]
        z = [sb(f"z{c}", [P, COLS]) for c in range(CHAINS)]
        one_z = [sb(f"one_z{c}", [P, COLS]) for c in range(CHAINS)]
        rh = [sb(f"rh{c}", [P, COLS]) for c in range(CHAINS)]
        pre = [sb(f"pre{c}", [P, COLS]) for c in range(CHAINS)]
        cand = [sb(f"cand{c}", [P, COLS]) for c in range(CHAINS)]
        zh = [sb(f"zh{c}", [P, COLS]) for c in range(CHAINS)]
        zc = [sb(f"zc{c}", [P, COLS]) for c in range(CHAINS)]
        logits = sb("logits", [P, BLOCKS, CLASSES])
        probs = sb("probs", [P, BLOCKS, CLASSES])
        top = sb("top", [P, BLOCKS])
        neg_top = sb("neg_top", [P, BLOCKS])
        total = sb("total", [P, BLOCKS])
        inv_total = sb("inv_total", [P, BLOCKS])

        bank = [ctx.enter_context(nc.psum_tensor(f"bank{i}", [P, 512], F32)) for i in range(8)]
        reset_bank = [bank[1], bank[5]]
        update_bank = [bank[2], bank[6]]
        cand_bank = [bank[3], bank[7]]
        emb_bank = bank[0:2]
        proj_bank = bank[2:6]

        s_seq = sem("seq_loaded")
        s_w = sem("W_loaded")
        s_params = sem("parameters_loaded")
        s_const = sem("constants_ready")
        s_ident0 = sem("ident_zeroed")
        s_ident = sem("ident_ready")
        s_idx = sem("index_steps")
        s_table_rows = sem("table_rows_ready")
        s_bias = sem("biases_ready")
        s_emb = [sem(f"emb_loaded{q}") for q in range(AHEAD)]
        s_embt = sem("emb_transposed")
        s_embc = sem("emb_t_copied")
        s_proj = sem("projected")
        s_pact = sem("proj_copied_scalar")
        s_pdve = sem("proj_copied_vector")
        s_store = [sem(f"table_stored{q}") for q in range(2)]
        s_padrow = sem("pad_row_stored")
        s_now = [sem(f"rows_staged{q}") for q in range(2)]
        s_slot = [per_chain(f"slot{s}_gathered") for s in range(RING)]
        s_free = per_chain("slots_free")
        s_paced = sem("gathers_paced")
        s_reset = per_chain("reset_summed")
        s_update = per_chain("update_summed")
        s_cand = per_chain("cand_summed")
        s_r = per_chain("r_ready")
        s_z = per_chain("z_ready")
        s_zz = per_chain("one_z_ready")
        s_rh = per_chain("rh_ready")
        s_pre = per_chain("pre_ready")
        s_tanh = per_chain("cand_ready")
        s_zc = per_chain("zc_ready")
        s_h = per_chain("h_ready")
        s_logit_ps = sem("logits_summed")
        s_logit = sem("logits_ready")
        s_top = sem("top_ready")
        s_ntop = sem("neg_top_ready")
        s_exp = sem("exp_ready")
        s_inv = sem("inv_ready")
        s_prob = sem("probs_ready")
        s_out = sem("out_stored")

        block = ctx.enter_context(nc.Block())

        def over_turns(eng, one_turn):
            one_turn(0)
            with eng.Fori(1, TURNS) as turn:
                one_turn(turn)

        def positive(x):
            return not isinstance(x, int) or x > 0

        def over_groups(eng, batch):
            batch(0)
            with eng.Fori(1, GROUPS // AHEAD - 1) as n:
                batch(n * AHEAD)
            batch(GROUPS - AHEAD)

        @block.sync
        def _(sp):
            def load_emb(g, q):
                sp.dma_start(emb_in[q][:, :].rearrange("p (j d) -> p j d", d=D),
                             emb_tiles[:, bass.ds(g * GROUP, GROUP), :]).then_inc(s_emb[q], 16)

            load_emb(0, 0)
            sp.dma_start(W_sb[:, :], W).then_inc(s_w, 16)
            for q in range(1, AHEAD):
                load_emb(q, q)
            sp.dma_start(seq[:, :, :], item_seq.rearrange("(k p) t -> p k t", p=P)).then_inc(s_seq, 16)
            for dst, src in ((U_sb, U), (bi, b_i), (br, b_r), (Wout_sb, Wout), (bout_sb, bout.partition_broadcast(P))):
                sp.dma_start(dst[:, :], src).then_inc(s_params, 16)
            sp.wait_ge(s_const, 1)
            sp.dma_start(table[ITEMS:ITEMS + 1, :], pad_row[:, :]).then_inc(s_padrow, 16)

            def store(g, p):
                sp.wait_ge(s_pact, (g + 1) * (GROUP // 2))
                sp.wait_ge(s_pdve, (g + 1) * (GROUP // 2))
                sp.dma_start(table_tiles[:, bass.ds(g * GROUP, GROUP), :], proj[p][:, :, :]).then_inc(s_store[p], 16)

            def batch(g):
                for q in range(AHEAD):
                    sp.wait_ge(s_embt, g + q + 1)
                    if not isinstance(g, int) or g + q + AHEAD < GROUPS:
                        load_emb(g + q + AHEAD, q)
                    elif g + q + AHEAD == GROUPS:
                        sp.dma_start(emb_in[0][:, 0:D], emb_tiles[:, TILES - 1, :]).then_inc(s_emb[0], 16)
                        sp.dma_start(emb_in[0][0:REST, D:2 * D], emb[TILES * P:ITEMS, :]).then_inc(s_emb[0], 16)
                    store(g + q, q % 2)

            over_groups(sp, batch)
            sp.wait_ge(s_pact, GROUPS * (GROUP // 2) + 1)
            sp.dma_start(table_tiles[:, TILES - 1, :], proj[0][:, 0, :]).then_inc(s_store[0], 16)
            sp.wait_ge(s_pdve, GROUPS * (GROUP // 2) + 1)
            sp.dma_start(table[TILES * P:ITEMS, :], proj[0][0:REST, 1, :]).then_inc(s_store[0], 16)

            def stage_rows(turn, q):
                sp.dma_start(row_now[:, q, :],
                             row_table[:, :, :].rearrange("p t k -> p (t k)")[
                                 :, bass.ds((turn * RING + q * HALF) * BLOCKS, HALF * BLOCKS)]
                             ).then_inc(s_now[q], 16)

            sp.wait_ge(s_table_rows, 1)
            stage_rows(0, 0)
            stage_rows(0, 1)
            with sp.Fori(1, TURNS) as turn:
                for q in range(2):
                    for s in range(q * HALF, (q + 1) * HALF):
                        for c in range(CHAINS):
                            sp.wait_ge(s_slot[s][c], turn * (16 * PER))
                    stage_rows(turn, q)

            sp.wait_ge(s_prob, BLOCKS)
            sp.dma_start(out.rearrange("(k p) n -> p k n", p=P), probs[:, :, :]).then_inc(s_out, 16)
            sp.wait_ge(s_out, 16)

        @block.gpsimd
        def _(pool):
            pool.memset(ident[:, :], 0.0).then_inc(s_ident0, 1)
            pool.wait_ge(s_ident0, 1)
            pool.affine_select(out=ident[:, :], in_=ident[:, :], compare_op=ALU.not_equal, fill=1.0,
                               base=0, pattern=[[-1, P]], channel_multiplier=1).then_inc(s_ident, 1)

            def gather(s, k, dst, src, rows):
                pool.indirect_dma_start(dst, None, src, bass.IndirectOffsetOnAxis(rows, 0)
                                        ).then_inc(s_slot[s][k // PER], 16)

            pool.wait_ge(s_store[0], 16 * (GROUPS // 2 + 2))
            pool.wait_ge(s_store[1], 16 * (GROUPS // 2))
            pool.wait_ge(s_padrow, 16)

            def one_turn(turn):
                for s in range(RING):
                    if s % HALF == 0:
                        pool.wait_ge(s_now[s // HALF], turn * 16 + 16)
                    for c in range(CHAINS):
                        if positive(turn):
                            pool.wait_ge(s_free[c], (turn - 1) * RING + s + 1)
                        pool.sem_inc(s_paced, 1)
                        for k in range(c * PER, (c + 1) * PER):
                            i = (s % HALF) * BLOCKS + k
                            gather(s, k, ring[:, s, k, :], table, row_now[:, s // HALF, i:i + 1])

            over_turns(pool, one_turn)

        @block.tensor
        def _(pe):
            def transpose_group(g, q, tiles=GROUP):
                if tiles == GROUP:
                    pe.wait_ge(s_emb[q], (g - q) * (16 // AHEAD) + 16)
                else:
                    pe.wait_ge(s_emb[q], 16 * (GROUPS // AHEAD + 2))
                if not isinstance(g, int) or g >= 2:
                    pe.wait_ge(s_embc, g - 1)
                for j in range(tiles):
                    n = P if tiles == GROUP or j == 0 else REST
                    last = pe.matmul(emb_bank[q % 2][:, j * P:j * P + n], emb_in[q][0:n, j * D:(j + 1) * D],
                                     ident[0:n, 0:n], start=(j == 0), stop=True, is_transpose=True,
                                     skip_group_check=True)
                last.then_inc(s_embt, 1)

            def project_group(g, p, tiles=GROUP):
                pe.wait_ge(s_embc, g + 1)
                for j in range(tiles):
                    n = P if tiles == GROUP or j == 0 else REST
                    if not isinstance(g, int) or g >= 1:
                        pe.wait_ge((s_pact, s_pdve)[j % 2], (g - 1) * (GROUP // 2) + j // 2 + 1)
                    pe.matmul(proj_bank[j][0:n, 0:GATES], emb_t[p][:, j * P:j * P + n], W_sb[:, :],
                              start=True, stop=True).then_inc(s_proj, 1)

            pe.wait_ge(s_ident, 1)
            transpose_group(0, 0)
            pe.wait_ge(s_w, 16)

            def batch(g):
                for q in range(AHEAD):
                    if isinstance(g, int) and g + q + 1 == GROUPS:
                        transpose_group(GROUPS, 0, 2)
                    else:
                        transpose_group(g + q + 1, (q + 1) % AHEAD)
                    project_group(g + q, q % 2)

            over_groups(pe, batch)
            project_group(GROUPS, 0, 2)

            def transpose_rows(turn, s, c):
                t = turn * RING + s
                pe.wait_ge(s_slot[s][c], (turn + 1) * (16 * PER))
                if positive(t):
                    pe.wait_ge(s_zz[c], t)
                    pe.wait_ge(s_pre[c], t)
                for dst, col, g in ((reset_bank[c], 0, 1), (cand_bank[c], COLS, 2), (update_bank[c], 0, 0)):
                    for b in range(PER):
                        last = pe.matmul(dst[:, col + b * P:col + (b + 1) * P],
                                         ring[:, s, c * PER + b, g * D:(g + 1) * D], ident[:, :],
                                         start=(b == 0), stop=False, is_transpose=True,
                                         skip_group_check=True)
                last.then_inc(s_free[c], 1)

            def recur(t, c):
                pe.wait_ge(s_h[c], t + 1)
                pe.matmul(reset_bank[c][:, 0:COLS], U_sb[:, D:2 * D], h[c][:, :], start=False,
                          stop=True, skip_group_check=True).then_inc(s_reset[c], 1)
                pe.matmul(cand_bank[c][:, 0:COLS], U_sb[:, 2 * D:3 * D], h[c][:, :], start=False,
                          stop=True, skip_group_check=True).then_inc(s_cand[c], 1)
                pe.matmul(update_bank[c][:, 0:COLS], U_sb[:, 0:D], h[c][:, :], start=False,
                          stop=True, skip_group_check=True).then_inc(s_update[c], 1)

            pe.wait_ge(s_pact, GROUPS * (GROUP // 2) + 1)
            pe.wait_ge(s_pdve, GROUPS * (GROUP // 2) + 1)
            pe.wait_ge(s_params, 16 * 5)

            def one_turn(turn):
                for s in range(RING):
                    for c in range(CHAINS):
                        transpose_rows(turn, s, c)
                        recur(turn * RING + s, c)

            over_turns(pe, one_turn)

            for k in range(BLOCKS):
                c, b = k // PER, k % PER
                if b == 0:
                    pe.wait_ge(s_h[c], STEPS + 1)
                last = pe.matmul(bank[0][:, k * CLASSES:(k + 1) * CLASSES], h[c][:, b * P:(b + 1) * P],
                                 Wout_sb[:, :], start=(k == 0), stop=True, skip_group_check=True)
            last.then_inc(s_logit_ps, 1)

        @block.scalar
        def _(act):
            def copy_proj(g, p, j):
                act.wait_ge(s_proj, g * GROUP + j + 1)
                if not isinstance(g, int) or g >= 2:
                    act.wait_ge(s_store[p], (g - p) * 8)
                act.copy(proj[p][:, j, :], proj_bank[j][:, 0:GATES]).then_inc(s_pact, 1)

            def batch(g):
                for q in range(AHEAD):
                    for j in range(0, GROUP, 2):
                        copy_proj(g + q, q % 2, j)

            over_groups(act, batch)
            copy_proj(GROUPS, 0, 0)

            def gates(t, c):
                act.wait_ge(s_reset[c], t + 1)
                act.activation(r[c][:, :], reset_bank[c][:, 0:COLS], ACT.Sigmoid,
                               bias=b_gates[:, 1:2]).then_inc(s_r[c], 1)
                act.wait_ge(s_update[c], t + 1)
                act.activation(z[c][:, :], update_bank[c][:, 0:COLS], ACT.Sigmoid,
                               bias=b_gates[:, 0:1]).then_inc(s_z[c], 1)
                act.activation(one_z[c][:, :], update_bank[c][:, 0:COLS], ACT.Sigmoid,
                               bias=b_keep[:, 0:1], scale=-1.0).then_inc(s_zz[c], 1)

            def candidate(t, c):
                act.wait_ge(s_pre[c], t + 1)
                act.activation(cand[c][:, :], pre[c][:, :], ACT.Tanh, bias=bi[:, 2:3]).then_inc(s_tanh[c], 1)

            act.wait_ge(s_bias, 1)

            def one_turn(turn):
                for s in range(RING):
                    for c in range(CHAINS):
                        gates(turn * RING + s, c)
                        candidate(turn * RING + s, c)

            over_turns(act, one_turn)

            act.wait_ge(s_ntop, 1)
            for k in range(BLOCKS):
                act.activation(probs[:, k, :], logits[:, k, :], ACT.Exp, bias=neg_top[:, k:k + 1],
                               accum_out=total[:, k:k + 1]).then_inc(s_exp, 1)

        @block.vector
        def _(dve):
            dve.memset(pad_row[:, :], 0.0).then_inc(s_idx, 1)
            for c in range(CHAINS):
                dve.memset(h[c][:, :], 0.0).then_inc(s_h[c], 1)
            dve.wait_ge(s_idx, 1)
            dve.memset(pad_row[:, 0:D], PINNED).then_inc(s_const, 1)

            dve.wait_ge(s_seq, 16)
            dve.tensor_scalar(row_f[:, :, :], seq[:, :, :], 0.0, float(ITEMS), ALU.is_lt, ALU.mult).then_inc(s_idx, 1)
            dve.wait_ge(s_idx, 2)
            dve.tensor_tensor(row_f[:, :, :], row_f[:, :, :], seq[:, :, :], ALU.add).then_inc(s_idx, 1)
            dve.wait_ge(s_idx, 3)
            dve.tensor_scalar(row_f[:, :, :], row_f[:, :, :], 0.0, float(ITEMS - 1), ALU.max, ALU.min).then_inc(s_idx, 1)
            dve.wait_ge(s_idx, 4)
            dve.tensor_scalar(pad_f[:, :, :], seq[:, :, :], 0.0, float(ITEMS), ALU.is_equal, ALU.mult).then_inc(s_idx, 1)
            dve.wait_ge(s_idx, 5)
            dve.tensor_tensor(row_table[:, :, :], row_f[:, :, :].rearrange("p k t -> p t k"),
                              pad_f[:, :, :].rearrange("p k t -> p t k"), ALU.add).then_inc(s_table_rows, 1)
            dve.wait_ge(s_params, 16 * 5)
            dve.tensor_tensor(b_gates[:, :], bi[:, 0:2], br[:, 0:2], ALU.add).then_inc(s_idx, 1)
            dve.wait_ge(s_idx, 6)
            dve.tensor_scalar(b_keep[:, :], b_gates[:, 0:1], -1.0, None, ALU.mult).then_inc(s_bias, 1)

            def copy_emb(g, p, cols=GROUP * P):
                dve.wait_ge(s_embt, g + 1)
                if not isinstance(g, int) or g >= 2:
                    dve.wait_ge(s_proj, (g - 1) * GROUP)
                dve.tensor_copy(emb_t[p][:, 0:cols], emb_bank[p][:, 0:cols]).then_inc(s_embc, 1)

            def copy_proj(g, p, j, n=P):
                dve.wait_ge(s_proj, g * GROUP + j + 1)
                if not isinstance(g, int) or g >= 2:
                    dve.wait_ge(s_store[p], (g - p) * 8)
                dve.tensor_copy(proj[p][0:n, j, :], proj_bank[j][0:n, 0:GATES]).then_inc(s_pdve, 1)

            copy_emb(0, 0)

            def batch(g):
                for q in range(AHEAD):
                    if isinstance(g, int) and g + q + 1 == GROUPS:
                        copy_emb(GROUPS, 0, P + REST)
                    else:
                        copy_emb(g + q + 1, (q + 1) % 2)
                    for j in range(1, GROUP, 2):
                        copy_proj(g + q, q % 2, j)

            over_groups(dve, batch)
            copy_proj(GROUPS, 0, 1, REST)
            def reset_h(t, c):
                dve.wait_ge(s_cand[c], t + 1)
                dve.wait_ge(s_r[c], t + 1)
                dve.scalar_tensor_tensor(out=rh[c][:, :], in0=cand_bank[c][:, 0:COLS],
                                         scalar=br[:, 2:3], in1=r[c][:, :], op0=ALU.add,
                                         op1=ALU.mult).then_inc(s_rh[c], 1)

            def add_x(t, c):
                dve.wait_ge(s_rh[c], t + 1)
                dve.tensor_tensor(pre[c][:, :], rh[c][:, :], cand_bank[c][:, COLS:2 * COLS],
                                  ALU.add).then_inc(s_pre[c], 1)

            def kept(t, c):
                dve.wait_ge(s_z[c], t + 1)
                dve.tensor_tensor(zh[c][:, :], z[c][:, :], h[c][:, :], ALU.mult)

            def added(t, c):
                dve.wait_ge(s_tanh[c], t + 1)
                dve.tensor_tensor(zc[c][:, :], one_z[c][:, :], cand[c][:, :], ALU.mult).then_inc(s_zc[c], 1)

            def new_h(t, c):
                dve.wait_ge(s_zc[c], t + 1)
                dve.tensor_tensor(h[c][:, :], zh[c][:, :], zc[c][:, :], ALU.add).then_inc(s_h[c], 1)

            def half_step(t, c, t_other):
                if t_other is not None:
                    added(t_other, 1 - c)
                reset_h(t, c)
                if t_other is not None:
                    new_h(t_other, 1 - c)
                add_x(t, c)
                kept(t, c)

            def one_turn(turn):
                for s in range(RING):
                    t = turn * RING + s
                    half_step(t, 0, t - 1 if positive(t) else None)
                    half_step(t, 1, t)

            over_turns(dve, one_turn)
            added(STEPS - 1, 1)
            new_h(STEPS - 1, 1)

            dve.wait_ge(s_logit_ps, 1)
            for k in range(BLOCKS):
                dve.tensor_tensor(logits[:, k, :], bank[0][:, k * CLASSES:(k + 1) * CLASSES],
                                  bout_sb[:, :], ALU.add).then_inc(s_logit, 1)
            dve.wait_ge(s_logit, BLOCKS)
            dve.tensor_reduce(top[:, :], logits[:, :, :], AX.X, ALU.max).then_inc(s_top, 1)
            dve.wait_ge(s_top, 1)
            dve.tensor_scalar(neg_top[:, :], top[:, :], -1.0, None, ALU.mult).then_inc(s_ntop, 1)
            dve.wait_ge(s_exp, BLOCKS)
            dve.reciprocal(inv_total[:, :], total[:, :]).then_inc(s_inv, 1)
            dve.wait_ge(s_inv, 1)
            for k in range(BLOCKS):
                dve.tensor_scalar(probs[:, k, :], probs[:, k, :], inv_total[:, k:k + 1], None,
                                  ALU.mult).then_inc(s_prob, 1)


_INS = ["r_item_seq", "L0_rec_emb", "L0_rec_W", "L0_rec_U", "L0_rec_b_i", "L0_rec_b_r", "L0_rec_Wout", "L0_rec_bout"]


def kernel(**inputs):
    import numpy as np
    import concourse.bacc as bacc
    from concourse.bass_utils import run_bass_kernel_spmd as run

    nc = bacc.Bacc("TRN2", target_bir_lowering=False, num_devices=1)
    arrays, args = {}, []
    for name in _INS:
        a = np.asarray(inputs[name])
        if name in ("L0_rec_b_i", "L0_rec_b_r"):
            a = a.reshape(3, -1).T
        a = np.ascontiguousarray(a)
        arrays[f"in_{name}"] = a
        args.append(nc.dram_tensor(f"in_{name}", a.shape, mybir.dt.from_np(a.dtype), kind="ExternalInput").ap())
    shape = (inputs["r_item_seq"].shape[0], inputs["L0_rec_Wout"].shape[1])
    out = nc.dram_tensor("out_probs", shape, F32, kind="ExternalOutput").ap()
    gru(nc, *args, out)
    return run(nc, [arrays], core_ids=[0]).results[0]["out_probs"]
```

```python
from contextlib import ExitStack

import concourse.bass as bass
from concourse import mybir

F32 = mybir.dt.float32
I32 = mybir.dt.int32
ALU = mybir.AluOpType
ACT = mybir.ActivationFunctionType
AX = mybir.AxisListType

P = 128
BLOCKS = 4
CHAINS = (((0, 0, 128), (1, 0, 64)), ((2, 0, 128), (1, 64, 128)), ((3, 0, 128),))
WIDTH = [sum(end - first for _, first, end in pieces) for pieces in CHAINS]
GATHERS = ((0, 1), (2,), (3,))
RING = 8
HALF = RING // 2
GROUP = 4
AHEAD = 4
PINNED = 1.0e30


def gru(nc: bass.Bass, item_seq, emb_cols, W, U, b_i, b_r, Wout, bout, out):
    BATCH, STEPS = item_seq.shape
    D, ITEMS = emb_cols.shape
    GATES = W.shape[1]
    CLASSES = Wout.shape[1]
    assert D == P and GATES == 3 * D and BATCH == BLOCKS * P and STEPS % RING == 0
    TURNS = STEPS // RING
    PIECES = sum(len(pieces) for pieces in CHAINS)
    TILES = ITEMS // P
    REST = ITEMS - TILES * P
    GROUPS = TILES // GROUP
    assert TILES == GROUPS * GROUP + 1 and 0 < REST < P and GROUPS % AHEAD == 0

    table = nc.dram_tensor("table", [ITEMS + 1, GATES], F32, kind="Internal").ap()
    table_tiles = table[0:TILES * P, :].rearrange("(p j) n -> p j n", j=TILES)

    with ExitStack() as ctx:
        def sb(name, shape, dt=F32):
            return ctx.enter_context(nc.sbuf_tensor(name, shape, dt))

        def sem(name):
            return ctx.enter_context(nc.semaphore(name))

        def per_chain(name):
            return [sem(f"{name}{c}") for c in range(len(CHAINS))]

        emb_in = [sb(f"emb_in{q}", [P, GROUP * P]) for q in range(AHEAD)]
        proj = [sb(f"proj{q}", [P, GROUP, GATES]) for q in range(AHEAD)]
        ring = sb("ring", [P, RING, BLOCKS, GATES])

        seq = sb("seq", [P, BLOCKS, STEPS], I32)
        item_f = sb("item_f", [P, BLOCKS, STEPS])
        row_f = sb("row_f", [P, BLOCKS, STEPS])
        pad_f = sb("pad_f", [P, BLOCKS, STEPS])
        row_table = sb("row_table", [P, STEPS, BLOCKS], I32)
        row_now = sb("row_now", [P, 2, HALF * BLOCKS], I32)
        pad_row = sb("pad_row", [1, GATES])
        ident = sb("ident", [P, P])
        W_sb = sb("W_sb", [P, GATES])
        U_sb = sb("U_sb", [P, GATES])
        Wout_sb = sb("Wout_sb", [P, CLASSES])
        bout_sb = sb("bout_sb", [P, CLASSES])
        bi = sb("bi", [P, 3])
        br = sb("br", [P, 3])
        b_gates = sb("b_gates", [P, 2])
        b_keep = sb("b_keep", [P, 1])
        h = [sb(f"h{c}", [P, n]) for c, n in enumerate(WIDTH)]
        r = [sb(f"r{c}", [P, n]) for c, n in enumerate(WIDTH)]
        z = [sb(f"z{c}", [P, n]) for c, n in enumerate(WIDTH)]
        one_z = [sb(f"one_z{c}", [P, n]) for c, n in enumerate(WIDTH)]
        rh = [sb(f"rh{c}", [P, n]) for c, n in enumerate(WIDTH)]
        pre = [sb(f"pre{c}", [P, n]) for c, n in enumerate(WIDTH)]
        cand = [sb(f"cand{c}", [P, n]) for c, n in enumerate(WIDTH)]
        zh = [sb(f"zh{c}", [P, n]) for c, n in enumerate(WIDTH)]
        zc = [sb(f"zc{c}", [P, n]) for c, n in enumerate(WIDTH)]
        logits = sb("logits", [P, PIECES, CLASSES])
        probs = sb("probs", [P, PIECES, CLASSES])
        top = sb("top", [P, PIECES])
        neg_top = sb("neg_top", [P, PIECES])
        total = sb("total", [P, PIECES])
        inv_total = sb("inv_total", [P, PIECES])

        bank = [ctx.enter_context(nc.psum_tensor(f"bank{i}", [P, 512], F32)) for i in range(8)]
        reset_sum = [bank[0][:, 0:WIDTH[0]], bank[3][:, 0:WIDTH[1]], bank[6][:, 0:WIDTH[2]]]
        update_sum = [bank[1][:, 0:WIDTH[0]], bank[4][:, 0:WIDTH[1]], bank[6][:, WIDTH[2]:2 * WIDTH[2]]]
        gates_share = [False, False, True]
        cand_h = [bank[b][:, 0:n] for b, n in zip((2, 5, 7), WIDTH)]
        cand_x = [bank[b][:, n:2 * n] for b, n in zip((2, 5, 7), WIDTH)]
        proj_bank = bank[0:GROUP]

        s_seq = sem("seq_loaded")
        s_w = sem("W_loaded")
        s_params = sem("parameters_loaded")
        s_const = sem("constants_ready")
        s_ident0 = sem("ident_zeroed")
        s_ident = sem("ident_ready")
        s_idx = sem("index_steps")
        s_setup = sem("setup_steps")
        s_table_rows = sem("table_rows_ready")
        s_bias = sem("biases_ready")
        s_emb = [sem(f"emb_loaded{q}") for q in range(AHEAD)]
        s_proj = sem("projected")
        s_pact = sem("proj_copied_scalar")
        s_pdve = sem("proj_copied_vector")
        s_store = [sem(f"table_stored{q}") for q in range(AHEAD)]
        s_padrow = sem("pad_row_stored")
        s_now = [sem(f"rows_staged{q}") for q in range(2)]
        s_slot = [[sem(f"slot{s}_block{k}_gathered") for k in range(BLOCKS)] for s in range(RING)]
        s_free = per_chain("rows_transposed")
        s_paced = sem("gathers_paced")
        s_reset = per_chain("reset_summed")
        s_update = per_chain("update_summed")
        s_cand = per_chain("cand_summed")
        s_r = per_chain("r_ready")
        s_z = per_chain("z_ready")
        s_rh = per_chain("rh_ready")
        s_pre = per_chain("pre_ready")
        s_tanh = per_chain("cand_ready")
        s_zc = per_chain("zc_ready")
        s_h = per_chain("h_ready")
        s_logit_ps = sem("logits_summed")
        s_logit = sem("logits_ready")
        s_top = sem("top_ready")
        s_ntop = sem("neg_top_ready")
        s_exp = sem("exp_ready")
        s_inv = sem("inv_ready")
        s_prob = sem("probs_ready")
        s_out = sem("out_stored")

        block = ctx.enter_context(nc.Block())

        def over_turns(eng, one_turn):
            one_turn(0)
            with eng.Fori(1, TURNS) as turn:
                one_turn(turn)

        def positive(x):
            return not isinstance(x, int) or x > 0

        def over_groups(eng, batch):
            batch(0)
            with eng.Fori(1, GROUPS // AHEAD - 1) as n:
                batch(n * AHEAD)
            batch(GROUPS - AHEAD)

        @block.sync
        def _(sp):
            def load_emb(g, q, cols=GROUP * P):
                sp.dma_start(emb_in[q][:, 0:cols], emb_cols[:, bass.ds(g * (GROUP * P), cols)]
                             ).then_inc(s_emb[q], 16)

            load_emb(0, 0)
            sp.dma_start(W_sb[:, :], W).then_inc(s_w, 16)
            for q in range(1, AHEAD):
                load_emb(q, q)
            sp.dma_start(seq[:, :, :], item_seq.rearrange("(k p) t -> p k t", p=P)).then_inc(s_seq, 16)
            for dst, src in ((U_sb, U), (bi, b_i), (br, b_r), (Wout_sb, Wout), (bout_sb, bout.partition_broadcast(P))):
                sp.dma_start(dst[:, :], src).then_inc(s_params, 16)
            sp.wait_ge(s_const, 1)
            sp.dma_start(table[ITEMS:ITEMS + 1, :], pad_row[:, :]).then_inc(s_padrow, 16)

            def store(g, q):
                sp.wait_ge(s_pact, (g + 1) * (GROUP // 2))
                sp.wait_ge(s_pdve, (g + 1) * (GROUP // 2))
                sp.dma_start(table_tiles[:, bass.ds(g * GROUP, GROUP), :], proj[q][:, :, :]
                             ).then_inc(s_store[q], 16)

            def batch(g):
                for q in range(AHEAD):
                    if not isinstance(g, int) or g + q + AHEAD <= GROUPS:
                        sp.wait_ge(s_proj, (g + q + 1) * GROUP)
                        last = isinstance(g, int) and g + q + AHEAD == GROUPS
                        load_emb(g + q + AHEAD, q, P + REST if last else GROUP * P)
                    store(g + q, q)

            over_groups(sp, batch)
            sp.wait_ge(s_pact, GROUPS * (GROUP // 2) + 1)
            sp.dma_start(table_tiles[:, TILES - 1, :], proj[0][:, 0, :]).then_inc(s_store[0], 16)
            sp.wait_ge(s_pdve, GROUPS * (GROUP // 2) + 1)
            sp.dma_start(table[TILES * P:ITEMS, :], proj[0][0:REST, 1, :]).then_inc(s_store[0], 16)

            def stage_rows(turn, q):
                sp.dma_start(row_now[:, q, :],
                             row_table[:, :, :].rearrange("p t k -> p (t k)")[
                                 :, bass.ds((turn * RING + q * HALF) * BLOCKS, HALF * BLOCKS)]
                             ).then_inc(s_now[q], 16)

            sp.wait_ge(s_table_rows, 1)
            stage_rows(0, 0)
            stage_rows(0, 1)
            with sp.Fori(1, TURNS) as turn:
                for q in range(2):
                    for s in range(q * HALF, (q + 1) * HALF):
                        for k in range(BLOCKS):
                            sp.wait_ge(s_slot[s][k], turn * 16)
                    stage_rows(turn, q)

            n = 0
            for pieces in CHAINS:
                for k, first, end in pieces:
                    sp.wait_ge(s_prob, n + 1)
                    sp.dma_start(out[k * P + first:k * P + end, :], probs[0:end - first, n, :]
                                 ).then_inc(s_out, 16)
                    n += 1
            sp.wait_ge(s_out, 16 * PIECES)

        @block.gpsimd
        def _(pool):
            pool.memset(ident[:, :], 0.0).then_inc(s_ident0, 1)
            pool.wait_ge(s_ident0, 1)
            pool.affine_select(out=ident[:, :], in_=ident[:, :], compare_op=ALU.not_equal, fill=1.0,
                               base=0, pattern=[[-1, P]], channel_multiplier=1).then_inc(s_ident, 1)

            pool.wait_ge(s_seq, 16)
            pool.tensor_copy(item_f[:, :, :], seq[:, :, :]).then_inc(s_idx, 1)
            pool.wait_ge(s_idx, 1)
            pool.tensor_scalar(row_f[:, :, :], item_f[:, :, :], 0.0, float(ITEMS), ALU.is_lt, ALU.mult
                               ).then_inc(s_idx, 1)
            pool.wait_ge(s_idx, 2)
            pool.tensor_tensor(row_f[:, :, :], row_f[:, :, :], item_f[:, :, :], ALU.add).then_inc(s_idx, 1)
            pool.tensor_scalar(pad_f[:, :, :], item_f[:, :, :], 0.0, float(ITEMS), ALU.is_equal, ALU.mult
                               ).then_inc(s_idx, 1)
            pool.wait_ge(s_idx, 4)
            pool.tensor_scalar(row_f[:, :, :], row_f[:, :, :], 0.0, float(ITEMS - 1), ALU.max, ALU.min
                               ).then_inc(s_idx, 1)
            pool.wait_ge(s_idx, 5)
            pool.tensor_tensor(row_f[:, :, :], row_f[:, :, :], pad_f[:, :, :], ALU.add).then_inc(s_idx, 1)
            pool.wait_ge(s_idx, 6)
            pool.tensor_copy(row_table[:, :, :], row_f[:, :, :].rearrange("p k t -> p t k")
                             ).then_inc(s_table_rows, 1)

            for q in range(AHEAD):
                pool.wait_ge(s_store[q], 16 * (GROUPS // AHEAD + (2 if q == 0 else 0)))
            pool.wait_ge(s_padrow, 16)

            def one_turn(turn):
                for s in range(RING):
                    if s % HALF == 0:
                        pool.wait_ge(s_now[s // HALF], turn * 16 + 16)
                    for c, blocks in enumerate(GATHERS):
                        if positive(turn) and c != 1:
                            pool.wait_ge(s_free[max(c, 1)], (turn - 1) * RING + s + 1)
                        pool.sem_inc(s_paced, 1)
                        for k in blocks:
                            i = (s % HALF) * BLOCKS + k
                            pool.indirect_dma_start(
                                ring[:, s, k, :], None, table,
                                bass.IndirectOffsetOnAxis(row_now[:, s // HALF, i:i + 1], 0)
                            ).then_inc(s_slot[s][k], 16)

            over_turns(pool, one_turn)

        @block.tensor
        def _(pe):
            def project_group(g, q, tiles=GROUP):
                pe.wait_ge(s_emb[q], (g - q) * (16 // AHEAD) + 16)
                for j in range(tiles):
                    n = P if tiles == GROUP or j == 0 else REST
                    if positive(g):
                        pe.wait_ge((s_pact, s_pdve)[j % 2], (g - 1) * (GROUP // 2) + j // 2 + 1)
                    pe.matmul(proj_bank[j][0:n, 0:GATES], emb_in[q][:, j * P:j * P + n], W_sb[:, :],
                              start=True, stop=True).then_inc(s_proj, 1)

            pe.wait_ge(s_w, 16)

            def batch(g):
                for q in range(AHEAD):
                    project_group(g + q, q)

            over_groups(pe, batch)
            project_group(GROUPS, 0, 2)

            def transpose_rows(turn, s, c):
                t = turn * RING + s
                for k in GATHERS[c]:
                    pe.wait_ge(s_slot[s][k], turn * 16 + 16)
                if positive(t):
                    pe.wait_ge(s_z[c], t)
                    pe.wait_ge(s_pre[c], t)
                col = 0
                for k, first, end in CHAINS[c]:
                    for dst, g in ((reset_sum[c], 1), (cand_x[c], 2), (update_sum[c], 0)):
                        opens = col == 0 and not (g == 0 and gates_share[c])
                        last = pe.matmul(dst[:, col:col + end - first], ring[first:end, s, k, g * D:(g + 1) * D],
                                         ident[first:end, first:end], start=opens, stop=False,
                                         is_transpose=True, skip_group_check=True)
                    col += end - first
                last.then_inc(s_free[c], 1)

            def add_h(dst, g, c, done):
                pe.matmul(dst, U_sb[:, g * D:(g + 1) * D], h[c][:, :], start=False, stop=True,
                          skip_group_check=True).then_inc(done, 1)

            def await_h(t, c):
                pe.wait_ge(s_h[c], t + 1)

            def reset_gate(c):
                add_h(reset_sum[c], 1, c, s_reset[c])

            def update_gate(c):
                add_h(update_sum[c], 0, c, s_update[c])

            def candidate(c):
                add_h(cand_h[c], 2, c, s_cand[c])

            pe.wait_ge(s_ident, 1)
            pe.wait_ge(s_params, 16 * 5)
            pe.wait_ge(s_pact, GROUPS * (GROUP // 2) + 1)
            pe.wait_ge(s_pdve, GROUPS * (GROUP // 2) + 1)

            def one_turn(turn):
                for s in range(RING):
                    t = turn * RING + s
                    transpose_rows(turn, s, 0)
                    transpose_rows(turn, s, 1)
                    await_h(t, 0)
                    reset_gate(0)
                    update_gate(0)
                    candidate(0)
                    transpose_rows(turn, s, 2)
                    await_h(t, 1)
                    reset_gate(1)
                    candidate(1)
                    update_gate(1)
                    await_h(t, 2)
                    candidate(2)
                    reset_gate(2)
                    update_gate(2)

            over_turns(pe, one_turn)

            n = 0
            for c, pieces in enumerate(CHAINS):
                pe.wait_ge(s_h[c], STEPS + 1)
                col = 0
                for _, first, end in pieces:
                    last = pe.matmul(bank[0][0:end - first, n * CLASSES:(n + 1) * CLASSES],
                                     h[c][:, col:col + end - first], Wout_sb[:, :], start=(n == 0),
                                     stop=True, skip_group_check=True)
                    col += end - first
                    n += 1
            last.then_inc(s_logit_ps, 1)

        @block.scalar
        def _(act):
            def copy_proj(g, q, j):
                act.wait_ge(s_proj, g * GROUP + j + 1)
                if not isinstance(g, int) or g >= AHEAD:
                    act.wait_ge(s_store[q], (g - q) * (16 // AHEAD))
                act.copy(proj[q][:, j, :], proj_bank[j][:, 0:GATES]).then_inc(s_pact, 1)

            def batch(g):
                for q in range(AHEAD):
                    for j in range(0, GROUP, 2):
                        copy_proj(g + q, q, j)

            over_groups(act, batch)
            copy_proj(GROUPS, 0, 0)

            def reset(t, c):
                act.wait_ge((s_update if gates_share[c] else s_reset)[c], t + 1)
                act.activation(r[c][:, :], reset_sum[c], ACT.Sigmoid, bias=b_gates[:, 1:2]).then_inc(s_r[c], 1)

            def one_less_update(t, c):
                if not gates_share[c]:
                    act.wait_ge(s_update[c], t + 1)
                act.activation(one_z[c][:, :], update_sum[c], ACT.Sigmoid, bias=b_keep[:, 0:1], scale=-1.0)

            def update(c):
                act.activation(z[c][:, :], update_sum[c], ACT.Sigmoid, bias=b_gates[:, 0:1]).then_inc(s_z[c], 1)

            def candidate(t, c):
                act.wait_ge(s_pre[c], t + 1)
                act.activation(cand[c][:, :], pre[c][:, :], ACT.Tanh, bias=bi[:, 2:3]).then_inc(s_tanh[c], 1)

            act.wait_ge(s_bias, 1)

            def one_turn(turn):
                for s in range(RING):
                    t = turn * RING + s
                    reset(t, 0)
                    one_less_update(t, 0)
                    update(0)
                    reset(t, 1)
                    candidate(t, 0)
                    one_less_update(t, 1)
                    update(1)
                    reset(t, 2)
                    one_less_update(t, 2)
                    candidate(t, 1)
                    update(2)
                    candidate(t, 2)

            over_turns(act, one_turn)

            n = 0
            for pieces in CHAINS:
                for _, first, end in pieces:
                    m = end - first
                    act.wait_ge(s_ntop, n + 1)
                    act.activation(probs[0:m, n, :], logits[0:m, n, :], ACT.Exp, bias=neg_top[0:m, n:n + 1],
                                   accum_out=total[0:m, n:n + 1]).then_inc(s_exp, 1)
                    n += 1

        @block.vector
        def _(dve):
            dve.memset(pad_row[:, :], 0.0).then_inc(s_setup, 1)
            for c in range(len(CHAINS)):
                dve.memset(h[c][:, :], 0.0).then_inc(s_h[c], 1)
            dve.wait_ge(s_setup, 1)
            dve.memset(pad_row[:, 0:D], PINNED).then_inc(s_const, 1)

            def copy_proj(g, q, j, n=P):
                dve.wait_ge(s_proj, g * GROUP + j + 1)
                if not isinstance(g, int) or g >= AHEAD:
                    dve.wait_ge(s_store[q], (g - q) * (16 // AHEAD))
                dve.tensor_copy(proj[q][0:n, j, :], proj_bank[j][0:n, 0:GATES]).then_inc(s_pdve, 1)

            def batch(g):
                for q in range(AHEAD):
                    for j in range(1, GROUP, 2):
                        copy_proj(g + q, q, j)

            over_groups(dve, batch)
            copy_proj(GROUPS, 0, 1, REST)

            dve.wait_ge(s_params, 16 * 5)
            dve.tensor_tensor(b_gates[:, :], bi[:, 0:2], br[:, 0:2], ALU.add).then_inc(s_setup, 1)
            dve.wait_ge(s_setup, 2)
            dve.tensor_scalar(b_keep[:, :], b_gates[:, 0:1], -1.0, None, ALU.mult).then_inc(s_bias, 1)

            def reset_h(t, c):
                dve.wait_ge(s_cand[c], t + 1)
                dve.wait_ge(s_r[c], t + 1)
                dve.scalar_tensor_tensor(out=rh[c][:, :], in0=cand_h[c],
                                         scalar=br[:, 2:3], in1=r[c][:, :], op0=ALU.add,
                                         op1=ALU.mult).then_inc(s_rh[c], 1)

            def add_x(t, c):
                dve.wait_ge(s_rh[c], t + 1)
                dve.tensor_tensor(pre[c][:, :], rh[c][:, :], cand_x[c],
                                  ALU.add).then_inc(s_pre[c], 1)

            def kept(t, c):
                dve.wait_ge(s_z[c], t + 1)
                dve.tensor_tensor(zh[c][:, :], z[c][:, :], h[c][:, :], ALU.mult)

            def added(t, c):
                dve.wait_ge(s_tanh[c], t + 1)
                dve.tensor_tensor(zc[c][:, :], one_z[c][:, :], cand[c][:, :], ALU.mult).then_inc(s_zc[c], 1)

            def new_h(t, c):
                dve.wait_ge(s_zc[c], t + 1)
                dve.tensor_tensor(h[c][:, :], zh[c][:, :], zc[c][:, :], ALU.add).then_inc(s_h[c], 1)

            def one_turn(turn):
                for s in range(RING):
                    t = turn * RING + s
                    if positive(t):
                        added(t - 1, 2)
                    reset_h(t, 0)
                    if positive(t):
                        new_h(t - 1, 2)
                    add_x(t, 0)
                    kept(t, 0)
                    reset_h(t, 1)
                    added(t, 0)
                    add_x(t, 1)
                    new_h(t, 0)
                    kept(t, 1)
                    reset_h(t, 2)
                    add_x(t, 2)
                    added(t, 1)
                    kept(t, 2)
                    new_h(t, 1)

            over_turns(dve, one_turn)
            added(STEPS - 1, 2)
            new_h(STEPS - 1, 2)

            rows = [end - first for pieces in CHAINS for _, first, end in pieces]
            dve.wait_ge(s_logit_ps, 1)
            for n, m in enumerate(rows):
                dve.tensor_tensor(logits[0:m, n, :], bank[0][0:m, n * CLASSES:(n + 1) * CLASSES],
                                  bout_sb[0:m, :], ALU.add).then_inc(s_logit, 1)
            for n, m in enumerate(rows):
                dve.wait_ge(s_logit, n + 1)
                dve.tensor_reduce(top[0:m, n:n + 1], logits[0:m, n, :], AX.X, ALU.max).then_inc(s_top, 1)
            for n, m in enumerate(rows):
                dve.wait_ge(s_top, n + 1)
                dve.tensor_scalar(neg_top[0:m, n:n + 1], top[0:m, n:n + 1], -1.0, None, ALU.mult
                                  ).then_inc(s_ntop, 1)
            for n, m in enumerate(rows):
                dve.wait_ge(s_exp, n + 1)
                dve.reciprocal(inv_total[0:m, n:n + 1], total[0:m, n:n + 1]).then_inc(s_inv, 1)
                dve.wait_ge(s_inv, n + 1)
                dve.tensor_scalar(probs[0:m, n, :], probs[0:m, n, :], inv_total[0:m, n:n + 1], None,
                                  ALU.mult).then_inc(s_prob, 1)


_INS = ["r_item_seq", "L0_rec_emb", "L0_rec_W", "L0_rec_U", "L0_rec_b_i", "L0_rec_b_r", "L0_rec_Wout", "L0_rec_bout"]


def kernel(**inputs):
    import numpy as np
    import concourse.bacc as bacc
    from concourse.bass_utils import run_bass_kernel_spmd as run

    nc = bacc.Bacc("TRN2", target_bir_lowering=False, num_devices=1)
    arrays, args = {}, []
    for name in _INS:
        a = np.asarray(inputs[name])
        if name == "L0_rec_emb":
            whole = a.shape[0] // P * P
            tiles = a[:whole].reshape(P, whole // P, -1).transpose(2, 1, 0)
            a = np.concatenate([tiles.reshape(a.shape[1], whole), a[whole:].T], axis=1)
        if name in ("L0_rec_b_i", "L0_rec_b_r"):
            a = a.reshape(3, -1).T
        a = np.ascontiguousarray(a)
        arrays[f"in_{name}"] = a
        args.append(nc.dram_tensor(f"in_{name}", a.shape, mybir.dt.from_np(a.dtype), kind="ExternalInput").ap())
    shape = (inputs["r_item_seq"].shape[0], inputs["L0_rec_Wout"].shape[1])
    out = nc.dram_tensor("out_probs", shape, F32, kind="ExternalOutput").ap()
    gru(nc, *args, out)
    return run(nc, [arrays], core_ids=[0]).results[0]["out_probs"]
```
